# Optimizing a Trainium2 kernel written in Bass

```python
import numpy as np
import jax
import jax.numpy as jnp

def _softmax(x, axis=-1):
    return jax.nn.softmax(x, axis=axis)

def _gelu(x):
    return jax.nn.gelu(x, approximate=True)

def _silu(x):
    return jax.nn.silu(x)

def _sigmoid(x):
    return jax.nn.sigmoid(x)

def _layernorm(x, axis=-1, eps=1e-05):
    m = jnp.mean(x, axis=axis, keepdims=True)
    v = jnp.var(x, axis=axis, keepdims=True)
    return (x - m) / jnp.sqrt(v + eps)

def _scatter_add(tgt, idx, src, axis=0):
    return tgt.at[idx].add(src)

def _segment_sum(src, seg, n):
    return jax.ops.segment_sum(src, seg, n)
kernel_name = 'mk_decoder_postln_d1_seqx_r8_86984d'

def setup_inputs(seed: int=0):
    np.random.seed(seed)
    _w = jnp.asarray

    def _rec_inputs():
        import jax
        import jax.numpy as jnp
        _rk = jax.random.key(seed)
        x = -0.0002928 + 1 * jax.random.normal(jax.random.fold_in(_rk, 1), (32, 56, 128), jnp.float32)
        _lenS = 56 - jax.random.randint(jax.random.fold_in(_rk, 7), (32,), 0, max(1, 56 // 4) + 1, jnp.int32)
        _lenS2 = 1500 - jax.random.randint(jax.random.fold_in(_rk, 8), (32,), 0, max(1, 1500 // 4) + 1, jnp.int32)
        _ctx_768P = jax.random.normal(jax.random.fold_in(_rk, 11), (32, 16, 96), jnp.float32)
        _ctx_768c = jax.random.dirichlet(jax.random.fold_in(_rk, 511), 0.3 * jnp.ones((16,), jnp.float32), (32, 1500))
        _ctx_768t = jnp.einsum('bsk,bkd->bsd', _ctx_768c, _ctx_768P)
        _ctx_768t = _ctx_768t * jax.lax.rsqrt(jnp.mean(jnp.square(_ctx_768t)) + 1e-12) * 0.953939
        ctx_768 = 2.09791e-05 + 1.00001 * (_ctx_768t + 0.3 * jax.random.normal(jax.random.fold_in(_rk, 611), (32, 1500, 96), jnp.float32))
        return (x, ctx_768)
    x, ctx_768 = _rec_inputs()

    def _L0_attn_setup():
        import jax, jax.numpy as jnp
        import numpy as np
        NUM_HEADS = 16
        NUM_GROUPS = 4
        GROUP_SIZE = NUM_HEADS // NUM_GROUPS
        EMB_DIM = 128
        HEAD_DIM = EMB_DIM // NUM_HEADS
        BLOCK_SIZE = 256
        B, T = (4, 256)
        key = jax.random.key(seed)
        ks = jax.random.split(key, 7)
        s = 0.02
        x = jax.random.normal(ks[0], (B, T, EMB_DIM), dtype=jnp.float32)
        Wq = jax.random.normal(ks[1], (NUM_HEADS, HEAD_DIM, EMB_DIM), dtype=jnp.float32) * s
        Wk = jax.random.normal(ks[2], (NUM_GROUPS, HEAD_DIM, EMB_DIM), dtype=jnp.float32) * s
        Wv = jax.random.normal(ks[3], (NUM_GROUPS, HEAD_DIM, EMB_DIM), dtype=jnp.float32) * s
        Wp = jax.random.normal(ks[4], (EMB_DIM, EMB_DIM), dtype=jnp.float32) * s
        bp = jax.random.normal(ks[5], (EMB_DIM,), dtype=jnp.float32) * s
        return {'x': x, 'Wq': Wq, 'Wk': Wk, 'Wv': Wv, 'Wp': Wp, 'bp': bp}
    _L0_attn_all = _L0_attn_setup()
    _L0_attn_in = {k: v for k, v in _L0_attn_all.items() if k in ('Wq', 'Wk', 'Wv', 'Wp', 'bp')}
    del _L0_attn_all

    def _L0_xattn_setup():
        import jax, jax.numpy as jnp
        import numpy as np
        H = 8
        D = 64
        SCALE = D ** (-0.5)
        key = jax.random.key(seed)
        ks = jax.random.split(key, 7)
        B, Nq, Nkv = (2, 256, 256)
        Cq, Ck, I = (128, 96, H * D)
        return {'x': jax.random.normal(ks[0], (B, Nq, Cq), jnp.float32), 'context': jax.random.normal(ks[1], (B, Nkv, Ck), jnp.float32), 'Wq': jax.random.normal(ks[2], (Cq, I), jnp.float32) * Cq ** (-0.5), 'Wk': jax.random.normal(ks[3], (Ck, I), jnp.float32) * Ck ** (-0.5), 'Wv': jax.random.normal(ks[4], (Ck, I), jnp.float32) * Ck ** (-0.5), 'Wo': jax.random.normal(ks[5], (I, Cq), jnp.float32) * I ** (-0.5), 'bo': jnp.zeros((Cq,), jnp.float32)}
    _L0_xattn_all = _L0_xattn_setup()
    _L0_xattn_in = {k: v for k, v in _L0_xattn_all.items() if k in ('Wq', 'Wk', 'Wv', 'Wo', 'bo')}
    del _L0_xattn_all

    def _L0_ffn_setup():
        import jax, jax.numpy as jnp
        import numpy as np
        B, S, H = (4, 256, 128)
        D = 256
        E = 8
        K = 2
        key = jax.random.key(seed)
        ks = jax.random.split(key, 8)
        w = lambda k, shape: jax.random.normal(k, shape, jnp.float32) * 0.02
        return {'hidden_states': jax.random.normal(ks[0], (B, S, H), jnp.float32), 'gate_w': w(ks[1], (H, E)), 'w_gate': w(ks[2], (E, H, D)), 'w_up': w(ks[3], (E, H, D)), 'w_down': w(ks[4], (E, D, H)), 'ws_gate': w(ks[5], (H, D)), 'ws_up': w(ks[6], (H, D)), 'ws_down': w(ks[7], (D, H))}
    _L0_ffn_all = _L0_ffn_setup()
    _L0_ffn_in = {k: v for k, v in _L0_ffn_all.items() if k in ('gate_w', 'w_gate', 'w_up', 'w_down', 'ws_gate', 'ws_up', 'ws_down')}
    del _L0_ffn_all
    return {'x': x, 'ctx_768': ctx_768, 'L0_attn_Wq': _L0_attn_in['Wq'], 'L0_attn_Wk': _L0_attn_in['Wk'], 'L0_attn_Wv': _L0_attn_in['Wv'], 'L0_attn_Wp': _L0_attn_in['Wp'], 'L0_attn_bp': _L0_attn_in['bp'], 'L0_xattn_Wq': _L0_xattn_in['Wq'], 'L0_xattn_Wk': _L0_xattn_in['Wk'], 'L0_xattn_Wv': _L0_xattn_in['Wv'], 'L0_xattn_Wo': _L0_xattn_in['Wo'], 'L0_xattn_bo': _L0_xattn_in['bo'], 'L0_ffn_gate_w': _L0_ffn_in['gate_w'], 'L0_ffn_w_gate': _L0_ffn_in['w_gate'], 'L0_ffn_w_up': _L0_ffn_in['w_up'], 'L0_ffn_w_down': _L0_ffn_in['w_down'], 'L0_ffn_ws_gate': _L0_ffn_in['ws_gate'], 'L0_ffn_ws_up': _L0_ffn_in['ws_up'], 'L0_ffn_ws_down': _L0_ffn_in['ws_down']}

def reference(x, ctx_768, L0_attn_Wq, L0_attn_Wk, L0_attn_Wv, L0_attn_Wp, L0_attn_bp, L0_xattn_Wq, L0_xattn_Wk, L0_xattn_Wv, L0_xattn_Wo, L0_xattn_bo, L0_ffn_gate_w, L0_ffn_w_gate, L0_ffn_w_up, L0_ffn_w_down, L0_ffn_ws_gate, L0_ffn_ws_up, L0_ffn_ws_down):
    import jax
    import jax.numpy as jnp

    def _L0_attn_ref(x, Wq, Wk, Wv, Wp, bp):
        import jax, jax.numpy as jnp
        import numpy as np
        NUM_HEADS = 16
        NUM_GROUPS = 4
        GROUP_SIZE = NUM_HEADS // NUM_GROUPS
        EMB_DIM = 128
        HEAD_DIM = EMB_DIM // NUM_HEADS
        BLOCK_SIZE = 256
        B, T = (4, 256)
        b, t, c = x.shape
        q = jnp.einsum('btc,hdc->bthd', x, Wq)
        k = jnp.einsum('btc,gdc->btgd', x, Wk)
        v = jnp.einsum('btc,gdc->btgd', x, Wv)
        k = jnp.repeat(k, GROUP_SIZE, axis=2)
        v = jnp.repeat(v, GROUP_SIZE, axis=2)
        scale = HEAD_DIM ** (-0.5)
        scores = jnp.einsum('bqhd,bkhd->bhqk', q, k) * scale
        causal = jnp.tril(jnp.ones((t, t), dtype=bool))
        scores = jnp.where(causal, scores, -jnp.inf)
        p = jax.nn.softmax(scores, axis=-1)
        out = jnp.einsum('bhqk,bkhd->bqhd', p, v)
        out = out.reshape(b, t, c)
        return out @ Wp.T + bp

    def _L0_xattn_ref(x, context, Wq, Wk, Wv, Wo, bo):
        import jax, jax.numpy as jnp
        import numpy as np
        H = 8
        D = 64
        SCALE = D ** (-0.5)
        B, Nq, _ = x.shape
        Nkv = context.shape[1]
        q = (x @ Wq).reshape(B, Nq, H, D)
        k = (context @ Wk).reshape(B, Nkv, H, D)
        v = (context @ Wv).reshape(B, Nkv, H, D)
        sim = jnp.einsum('bihd,bjhd->bhij', q, k) * SCALE
        attn = jax.nn.softmax(sim, axis=-1)
        out = jnp.einsum('bhij,bjhd->bihd', attn, v).reshape(B, Nq, H * D)
        return out @ Wo + bo

    def _L0_ffn_ref(hidden_states, gate_w, w_gate, w_up, w_down, ws_gate, ws_up, ws_down):
        import jax, jax.numpy as jnp
        import numpy as np
        B, S, H = (4, 256, 128)
        D = 256
        E = 8
        K = 2
        b, s, h = hidden_states.shape
        x = hidden_states.reshape(-1, h)
        scores = jax.nn.softmax(x @ gate_w, axis=-1)
        topk_w, topk_idx = jax.lax.top_k(scores, K)
        topk_w = topk_w / (jnp.sum(topk_w, axis=-1, keepdims=True) + 1e-20)
        onehot = jax.nn.one_hot(topk_idx, E, dtype=x.dtype)
        w_per_expert = jnp.einsum('nke,nk->ne', onehot, topk_w)
        y = jnp.zeros_like(x)
        for e in range(E):
            hid = jax.nn.silu(x @ w_gate[e]) * (x @ w_up[e])
            y = y + w_per_expert[:, e:e + 1] * (hid @ w_down[e])
        shared = jax.nn.silu(x @ ws_gate) * (x @ ws_up) @ ws_down
        return (y + shared).reshape(b, s, h)
    x = _layernorm(x + _L0_attn_ref(x, L0_attn_Wq, L0_attn_Wk, L0_attn_Wv, L0_attn_Wp, L0_attn_bp), axis=-1)
    x = _layernorm(x + _L0_xattn_ref(x, ctx_768, L0_xattn_Wq, L0_xattn_Wk, L0_xattn_Wv, L0_xattn_Wo, L0_xattn_bo), axis=-1)
    x = _layernorm(x + _L0_ffn_ref(x, L0_ffn_gate_w, L0_ffn_w_gate, L0_ffn_w_up, L0_ffn_w_down, L0_ffn_ws_gate, L0_ffn_ws_up, L0_ffn_ws_down), axis=-1)
    return x

_drawn_inputs = setup_inputs


def setup_inputs(seed=0):
    import zlib

    import numpy as np

    out = dict(_drawn_inputs(seed))
    spreads = {'L0_xattn_bo': (0.0, 0.1)}
    factors = {'L0_attn_Wq': 8.0,
     'L0_attn_Wk': 8.0,
     'L0_attn_Wv': 4.304,
     'L0_attn_Wp': 4.287,
     'L0_ffn_gate_w': 8.0,
     'L0_ffn_w_gate': 8.0,
     'L0_ffn_w_up': 8.0,
     'L0_ffn_w_down': 8.0,
     'L0_ffn_ws_gate': 6.944,
     'L0_ffn_ws_up': 6.833,
     'L0_ffn_ws_down': 6.877}
    for name, (base, spread) in spreads.items():
        noise = np.random.default_rng([zlib.crc32(name.encode()), seed]).standard_normal(out[name].shape)
        drawn = base * np.exp(spread * noise) if base else spread * noise
        out[name] = jnp.asarray(drawn.astype(out[name].dtype))
    for name, factor in factors.items():
        out[name] = (out[name] * factor).astype(out[name].dtype)
    return out
```

```python
from contextlib import ExitStack

import numpy as np
import concourse.bass as bass
from concourse import mybir

ALU = mybir.AluOpType
ACT = mybir.ActivationFunctionType
F32 = mybir.dt.float32
F32R = mybir.dt.float32r
BF16 = mybir.dt.bfloat16
U32 = mybir.dt.uint32
AX = mybir.AxisListType

B, T, C = 32, 56, 128
PT = 2 * T
PAIRS = B // 2
KV, CX = 1500, 96
KT, NT = 125, 12
CHUNK = 4 * KT
XH, XD = 8, 64
XR = XH * T
SH, SG, SJ, SD = 16, 4, 4, 8
EX, ED = 8, 256
FB = 448
NB = B * T // FB
PPB = FB // PT
EPS = 1e-5
S_SCALE = SD ** -0.5
X_SCALE = XD ** -0.5
MASKED = -1e30
MAX_ROW = 24

SIDE = [(0, "S3", "second"), (1, "S3", "second"), (2, "S4", "second"), (4, "S5", "second"),
        (5, "Y0", "post"), (6, "S6", "second"), (7, "Y1", "post"), (8, "S7", "second"),
        (9, "mrow", "main"), (10, "S8", "second"), (11, "Y2", "post"), (12, "S0q", "first"),
        (13, "S0k", "first"), (14, "S1", "first"), (15, "S1", "first"), (16, "S1", "first"),
        (17, "S1", "first"), (18, "X2T", "post"), (19, "S2", "first"), (20, "S3", "first"),
        (21, "mrow", "second"), (22, "S8", "second"), (23, "S3", "first")]
S1_GROUP = {14: 0, 15: 1, 16: 2, 17: 3}
S3_GROUP = {20: 0, 23: 1, 0: 2, 1: 3}
Y_HEADS = {5: (0, 1, 2), 7: (3, 4, 5), 11: (6, 7)}
MAXIMA = {1: (0, 1), 2: (2,), 3: (3, 4), 4: (5,), 5: (6, 7), 6: (8,), 7: (9, 10), 8: (11,)}
LOOP_FROM, LOOP_TO = 2, PAIRS - 2


def parts(i):
    if not isinstance(i, int):
        return {"main", "post", "second", "first"}
    return {name for name, lo, hi in (("main", 0, PAIRS), ("post", 1, PAIRS + 1),
                                      ("second", -1, PAIRS - 1), ("first", -2, PAIRS - 2))
            if lo <= i < hi}


def side_count(i, step):
    here = sum(1 for s, _, part in SIDE if s < step and part in parts(i))
    if not isinstance(i, int):
        return len(SIDE) * i + (side_count(LOOP_FROM, 0) - len(SIDE) * LOOP_FROM + here)
    return here + sum(1 for j in range(-2, i) for _, _, part in SIDE if part in parts(j))


def side_count_before(i, step):
    if isinstance(i, int):
        return side_count(i - 1, step)
    return side_count(i, 0) - sum(1 for s, _, _ in SIDE if s >= step)


SIDE_END = side_count(PAIRS + 1, 0)
SPLIT_STEPS = [(-2, 16), (-2, 23), (-1, 3)]
EXPERTS = (EX,) + tuple(range(EX))
UNITS = 2 * len(EXPERTS)
GATE_STEPS = 21
CONST_COLS = 128 + 3 + 2 * PT + EX


def bass_decoder_layer(nc, x_t, x_n, ctx_n, ctx_t, s_wq_t, s_wkv_t, s_wp_t, s_bias, x_wq_t, x_wk_t, x_wv_t,
                       x_wo, gate_w, w_gate, w_up, w_down, consts, out):
    with ExitStack() as ctx:
        def sb(name, shape, dt=F32):
            return ctx.enter_context(nc.sbuf_tensor(name, shape, dt))

        def ps(name, shape):
            return ctx.enter_context(nc.psum_tensor(name, shape, F32))

        def sem(name):
            return ctx.enter_context(nc.semaphore(name))

        cst = sb("cst", [128, CONST_COLS])
        ident = cst[:, 0:128]
        q_part, k_part, k_ones = (cst[:, 128 + n:129 + n] for n in range(3))
        iota8 = cst[0:PT, 131 + 2 * PT:139 + 2 * PT]
        ident_b = sb("ident_b", [128, PT], BF16)
        mask_b = sb("mask_b", [PT, 2, SJ, PT], BF16)
        eps = sb("eps", [128, 4])
        nhalf = sb("nhalf", [128, 4])
        spare = sb("spare", [128, 32])
        taken = [0]
        swq = sb("swq", [128, SG, SJ, SD])
        swkv = sb("swkv", [128, 2, SG, SD])
        swp = sb("swp", [128, C])
        bias2 = sb("bias2", [PT, 2, C])
        wq_pad = sb("wq_pad", [128, SJ, SG, 32])
        wk_pad = sb("wk_pad", [128, SG, 32])
        qk_prod = sb("qk_prod", [128, XH, CX])
        vo_prod = sb("vo_prod", [CX + 1, XH, C + 1])
        gw = sb("gw", [128, EX])
        gw_hl = [sb(f"gw_{p}", [128, EX], F32R) for p in ("hi", "lo")]
        wsp = [[sb(f"w_{n}_{p}", [128, (EX + 1) * ED], F32R) for p in ("hi", "lo")] for n in ("gate", "up", "down")]
        x_all = sb("x_all", [128, (EX + 1) * ED])
        x_rows = x_all[0:PT, 0:PAIRS * C]
        x2t = [sb(f"x2t_{p}", [128, B * T], F32R) for p in ("hi", "lo")]
        xt = sb("xt", [128, PT])
        xn = sb("xn", [PT, C])
        xr = sb("xr", [PT, C])
        q_hi = sb("q_hi", [128, SJ * PT], F32R)
        q_s = sb("q_s", [128, SJ * PT], F32R)
        q_m = sb("q_m", [128, SJ * PT], F32R)
        k_hi = sb("k_hi", [128, PT], F32R)
        k_s = sb("k_s", [128, PT], F32R)
        v_s = sb("v_s", [PT, SG, SD + 1])
        m_pl = sb("m_pl", [128, SJ, 128])
        p_s = sb("p_s", [128, SG, SJ * PT])
        rl_s = sb("rl_s", [PT, SH])
        o_s = sb("o_s", [PT, C])
        o_t = sb("o_t", [C, PT])
        r1 = sb("r1", [PT, C])
        st1 = sb("st1", [PT, 6])
        mv1 = sb("mv1", [PT, 2])
        rstd1 = sb("rstd1", [PT, 2])
        x1 = sb("x1", [PT, C])
        x1t = sb("x1t", [C, PT])
        ct_raw = sb("ct_raw", [128, 3, CHUNK])
        ct_hi = sb("ct_hi", [CX + 1, 2, 3 * CHUNK], F32R)
        ct_lo = sb("ct_lo", [CX, 2, 3 * CHUNK], F32R)
        v_raw = sb("v_raw", [128, NT * CX])
        v_raw_t = v_raw[0:KT, :].rearrange("p (t c) -> p t c", t=NT)
        v_hi = sb("v_hi", [KT, 2, NT, CX + 1], F32R)
        v_lo = sb("v_lo", [KT, 2, NT, CX], F32R)
        qa_hi = sb("qa_hi", [CX, XR], F32R)
        qa_lo = sb("qa_lo", [CX, XR], F32R)
        qb_hi = sb("qb_hi", [CX + 1, 2, XR], F32R)
        qb_lo = sb("qb_lo", [CX, 2, XR], F32R)
        mx = sb("mx", [PT, 4, 3])
        negm = sb("negm", [PT, 4])
        p_hi = [sb(f"p_hi{n}", [128, 2, XR], F32R) for n in range(3)]
        p_lo = [sb(f"p_lo{n}", [128, 2, XR], F32R) for n in range(3)]
        u_s = sb("u_s", [128, XH, PT])
        ry = sb("ry", [PT, 4])
        acc = sb("acc", [PT, C])
        st2 = sb("st2", [PT, 6])
        mv2 = sb("mv2", [PT, 2])
        rstd2 = sb("rstd2", [PT, 2])
        x2 = sb("x2", [PT, C])
        ct_flat = ct_raw[:, :, :].rearrange("p c n -> p (c n)")
        u_flat = u_s[:, :, :].rearrange("p h n -> p (h n)")
        p_flat = p_s[0:PT, :, :].rearrange("p g n -> p (g n)")
        silu_s = ct_flat[:, 0:2 * FB].rearrange("p (k n) -> p k n", k=2)
        lg_t = silu_s[0:EX, :, :]
        hid = v_raw[:, 0:2 * FB].rearrange("p (k n) -> p k n", k=2)
        wgt_b = u_flat[:, 0:2 * FB].rearrange("p (k n) -> p k n", k=2)
        y_t = m_pl[:, :, :].rearrange("p j n -> p (j n)")[:, 0:FB]
        wt_hl = ct_hi[0:2 * EX, :, :].rearrange("p c n -> p (c n)")[:, 0:B * T]
        sel = ct_lo[0:2 * EX, :, :].rearrange("p c n -> p (c n)")[:, 0:EX * 128].rearrange("p (e m) -> p e m", e=EX)
        gt = p_flat[:, 0:8 * PAIRS * EX].rearrange("p (k q e) -> p k q e", k=8, e=EX)
        w_hl = p_flat[:, 8 * PAIRS * EX:10 * PAIRS * EX].rearrange("p (q e) -> p q e", q=PAIRS)
        g1 = sb("g1", [PT, 7, PAIRS])
        gi = sb("gi", [PT, PAIRS, 8], U32)
        w_h = sb("w_h", [PT, PAIRS, EX], F32R)
        fin = sb("fin", [PT, PPB, C])
        out_s = sb("out_s", [PT, PPB, C])
        st3 = sb("st3", [PT, PPB, 6])
        mv3 = sb("mv3", [PT, PPB, 2])
        rstd3 = sb("rstd3", [PT, 2, PPB])
        wq_f = p_s[0:XD, :, :].rearrange("p g n -> p (g n)")[:, 0:XH * C].rearrange("p (h c) -> p h c", h=XH)
        wk_f = p_s[0:XD, :, :].rearrange("p g n -> p (g n)")[:, XH * C:XH * (C + CX)].rearrange("p (h c) -> p h c", h=XH)
        wv_f = u_flat[0:XD, 0:XH * CX].rearrange("p (h c) -> p h c", h=XH)
        wo_f = v_raw[0:XD, 0:XH * C].rearrange("p (h c) -> p h c", h=XH)

        ps_a = [ps(f"ps_a{n}", [128, 512]) for n in range(2)]
        ps_b = [ps(f"ps_b{n}", [128, 2, 512]) for n in range(2)]
        ps_u = ps("ps_u", [128, 512])
        side = ps("side", [128, 512])

        cst_ld, sw_ld, xw_ld, swp_ld, bias_ld, gw_ld, w_ld, xt_ld, xn_ld, v_ld, out_st = (sem(n) for n in (
            "cst_ld", "sw_ld", "xw_ld", "swp_ld", "bias_ld", "gw_ld", "w_ld", "xt_ld", "xn_ld", "v_ld", "out_st"))
        ct_ld = [sem(f"ct_ld{c}") for c in range(3)]
        zeroed, pads_set, masks_set, prod_full, qk_set, vo_set, w_hi_set, w_split = (sem(n) for n in (
            "zeroed", "pads_set", "masks_set", "prod_full", "qk_set", "vo_set", "w_hi_set", "w_split"))
        side_full, side_free = sem("side_full"), sem("side_free")
        rows_set = sem("rows_set")
        a_full, a_max, b_full, pv_done = (sem(n) for n in ("a_full", "a_max", "b_full", "pv_done"))
        exp_hi, exp_raw, plo_set = (sem(n) for n in ("exp_hi", "exp_raw", "plo_set"))
        negm_set, qa_hi_set, qb_set, u_set = (sem(n) for n in ("negm_set", "qa_hi_set", "qb_set", "u_set"))
        cthi_set, ctlo_set, vhi_set, vlo_set = (sem(n) for n in ("cthi_set", "ctlo_set", "vhi_set", "vlo_set"))
        q_hi_set, k_hi_set, rl_set, st1_set, mv1_set, ve1_set, rstd1_set, x1_set, xr_set, xb_set = (sem(n) for n in (
            "q_hi_set", "k_hi_set", "rl_set", "st1_set", "mv1_set", "ve1_set", "rstd1_set", "x1_set", "xr_set", "xb_set"))
        acc_init, ry_set, acc_set, st2_set, mv2_set, ve2_set, rstd2_set, x2_set, x2_kept, x2t_hi_set = (
            sem(n) for n in ("acc_init", "ry_set", "acc_set", "st2_set", "mv2_set", "ve2_set", "rstd2_set", "x2_set",
                             "x2_kept", "x2t_hi_set"))
        gw_hi_set, gw_lo_set, sel_set, lg_full, lg_set, gate_step, gate_exp, wt_full, wt_set = (sem(n) for n in (
            "gw_hi_set", "gw_lo_set", "sel_set", "lg_full", "lg_set", "gate_step", "gate_exp", "wt_full", "wt_set"))
        g_full, up_full, wb_full, wb_set, silu_set, weighted, hid_set, hid_hi_set, hid_lo_set, down_done = (
            sem(n) for n in ("g_full", "up_full", "wb_full", "wb_set", "silu_set", "weighted", "hid_set", "hid_hi_set",
                             "hid_lo_set", "down_done"))
        y_set, fin_full, fin_set, st3_set, mv3_set, ve3_set, rstd3_set, out_set = (sem(n) for n in (
            "y_set", "fin_full", "fin_set", "st3_set", "mv3_set", "ve3_set", "rstd3_set", "out_set"))

        def bits(ap):
            return ap.bitcast(F32)

        def over(ap, shape):
            return ap.broadcast_to(shape)

        def iterate(eng, body, first, loop_from, loop_to, last):
            for i in range(first, loop_from):
                body(i)
            with eng.Fori(loop_from, loop_to) as i:
                body(i)
            for i in range(loop_to, last):
                body(i)

        def exists(n, count=B, first=0):
            return not isinstance(n, int) or first <= n < count

        def wait(eng, s, n):
            if not isinstance(n, int) or n > 0:
                eng.wait_ge(s, n)

        def take_wait(eng):
            if eng is nc.vector:
                nc.vector.memset(spare[:, 0:1], 0.0)
            else:
                taken[0] = taken[0] % 31 + 1
                nc.gpsimd.tensor_tensor(spare[:, taken[0]:taken[0] + 1], eps[:, 0:1], eps[:, 0:1], ALU.add)

        block = ctx.enter_context(nc.Block())

        @block.sync
        def _(sp):
            sp.dma_start(cst[:, :], consts).then_inc(cst_ld, 16)
            sp.dma_start(swq[:, :, :, :], s_wq_t.rearrange("c (g j d) -> c g j d", g=SG, j=SJ)).then_inc(sw_ld, 16)
            sp.dma_start(swkv[:, :, :, :], s_wkv_t.rearrange("c (n g d) -> c n g d", n=2, g=SG)).then_inc(sw_ld, 16)
            sp.dma_start(xt[:, :], x_t[:, 0:PT]).then_inc(xt_ld, 16)
            sp.dma_start(x_all[:, :], w_gate).then_inc(w_ld, 16)
            for dst, src in ((wq_f, x_wq_t), (wk_f, x_wk_t), (wv_f, x_wv_t), (wo_f, x_wo)):
                sp.dma_start(dst, src.rearrange("(h d) c -> d h c", h=XH)).then_inc(xw_ld, 16)
            for c in range(3):
                sp.dma_start(ct_raw[0:CX, c, :], ctx_t[0:CX, c * CHUNK:(c + 1) * CHUNK]).then_inc(ct_ld[c], 16)
            sp.dma_start(xn[:, :], x_n[0:PT, :]).then_inc(xn_ld, 16)
            sp.dma_start(swp[:, :], s_wp_t).then_inc(swp_ld, 16)
            sp.dma_start(bias2[:, :, :], s_bias.rearrange("p (n c) -> p n c", n=2)).then_inc(bias_ld, 16)
            sp.dma_start(gw[:, :], gate_w).then_inc(gw_ld, 16)
            sp.wait_ge(prod_full, 2)
            sp.dma_start(v_raw_t, ctx_n[0:KT, :].rearrange("p (t c) -> p t c", t=NT)).then_inc(v_ld, 16)

            def body(i):
                if isinstance(i, int) and i == -2:
                    sp.wait_ge(side_free, side_count(-2, 13) + 1)
                    sp.dma_start(xt[:, :], x_t[:, PT:2 * PT]).then_inc(xt_ld, 16)
                    for n, src in ((1, w_up), (2, w_down)):
                        sp.wait_ge(w_split, n)
                        sp.dma_start(x_all[:, :], src).then_inc(w_ld, 16)
                    return
                for s in range(2):
                    n = 2 * i + s
                    if exists(n + 2, first=1):
                        wait(sp, ctlo_set, 3 * (n + 1) + 3)
                        sp.dma_start(ct_raw[0:CX, 2, :], ctx_t[bass.ds((n + 2) * CX, CX), 2 * CHUNK:3 * CHUNK])\
                          .then_inc(ct_ld[2], 16)
                    if s == 0 and exists(i + 2, PAIRS):
                        wait(sp, xr_set, i + 2)
                        sp.dma_start(xn[:, :], x_n[bass.ds((i + 2) * PT, PT), :]).then_inc(xn_ld, 16)
                    for c in range(2):
                        if exists(n + 3, first=1):
                            wait(sp, ctlo_set, 3 * (n + 2) + c + 1)
                            sp.dma_start(ct_raw[0:CX, c, :],
                                         ctx_t[bass.ds((n + 3) * CX, CX), c * CHUNK:(c + 1) * CHUNK])\
                              .then_inc(ct_ld[c], 16)
                        if c == 0 and exists(n + 2, first=1):
                            wait(sp, vlo_set, n + 2)
                            sp.dma_start(v_raw_t, ctx_n[bass.ds((n + 2) * KT, KT), :]
                                         .rearrange("p (t c) -> p t c", t=NT)).then_inc(v_ld, 16)
                    if s == 1 and exists(i + 3, PAIRS):
                        sp.wait_ge(side_free, side_count(i, 13) + 1)
                        sp.dma_start(xt[:, :], x_t[:, bass.ds((i + 3) * PT, PT)]).then_inc(xt_ld, 16)

            iterate(sp, body, -2, LOOP_FROM, PAIRS - 3, PAIRS)

            def store(c):
                sp.wait_ge(out_set, PPB * (c + 1))
                sp.dma_start(out[bass.ds(c * FB, FB), :].rearrange("(q p) n -> p q n", p=PT),
                             out_s[:, :, :]).then_inc(out_st, 16)

            iterate(sp, store, 0, 0, NB, NB)
            sp.wait_ge(out_st, 16 * NB)

        @block.tensor
        def _(pe):
            mm = nc.tensor.matmul

            def three(dst, weights, moving, first=True, last=True, short=None):
                w_lo_dst, w_lo_moving = (dst, moving[0]) if short is None else short
                mm(dst, weights[0], moving[0], start=first, stop=False, skip_group_check=True)
                mm(dst if short is None else dst, weights[0], moving[1], start=False, stop=False, skip_group_check=True)
                return mm(w_lo_dst, weights[1], w_lo_moving, start=False, stop=last, skip_group_check=True)

            pe.wait_ge(xw_ld, 64)
            for h in range(XH):
                ins = mm(ps_b[0][:, h // 4, (h % 4) * CX:(h % 4 + 1) * CX], wq_f[:, h, :], wk_f[:, h, :],
                         start=True, stop=True)
            ins.then_inc(prod_full, 1)
            for h in range(XH):
                ins = mm(ps_b[1][0:CX, h // 4, (h % 4) * C:(h % 4 + 1) * C], wv_f[:, h, :], wo_f[:, h, :],
                         start=True, stop=True)
            ins.then_inc(prod_full, 1)

            def maxima(n, k):
                chunk, rows = k // 4, k % 4
                if k == 0:
                    pe.wait_ge(qa_hi_set, n + 1)
                if rows == 0:
                    pe.wait_ge(cthi_set, 3 * n + chunk + 1)
                wait(pe, a_max, 12 * n + k - 1)
                mm(ps_a[k % 2][0:PT, 0:CHUNK], qa_hi[:, rows * PT:(rows + 1) * PT],
                   ct_hi[0:CX, k_seq(n), chunk * CHUNK:(chunk + 1) * CHUNK], start=True, stop=True).then_inc(a_full, 1)

            def scores(i, s, t):
                n, u = 2 * i + s, t // 2
                if t == 0:
                    pe.wait_ge(qb_set, n + 1)
                    pe.wait_ge(side_free, (side_count(i, 9) if s else side_count_before(i, 21)) + 1)
                if t == 0 and isinstance(i, int) and i == 0 and s == 0:
                    pe.wait_ge(qk_set, 1)
                    pe.wait_ge(vo_set, 1)
                if t % 4 == 0:
                    pe.wait_ge(ctlo_set, 3 * n + t // 4 + 1)
                if t % 2 == 0:
                    wait(pe, plo_set, 6 * n + u - 1)
                dst = ps_b[u % 2][0:KT, t % 2, 0:XR]
                keys = slice(t * KT, (t + 1) * KT)
                mm(dst, ct_hi[:, s, keys], qb_hi[:, s, :], start=True, stop=False)
                mm(dst, ct_hi[0:CX, s, keys], qb_lo[:, s, :], start=False, stop=False)
                ins = mm(dst, ct_lo[:, s, keys], qb_hi[0:CX, s, :], start=False, stop=True)
                if t % 2:
                    ins.then_inc(b_full, 1)

            def sums(n, s, u, k):
                t = 2 * u + k
                if k == 0:
                    pe.wait_ge(plo_set, 6 * n + u + 1)
                if t == 0:
                    pe.wait_ge(vlo_set, n + 1)
                    wait(pe, u_set, n)
                mm(ps_u[0:CX + 1, 0:XR], v_hi[:, s, t, :], p_hi[u % 3][0:KT, k, :],
                   start=(t == 0), stop=False, skip_group_check=True)
                mm(ps_u[0:CX + 1, 0:XR], v_hi[:, s, t, :], p_lo[u % 3][0:KT, k, :],
                   start=False, stop=False, skip_group_check=True)
                ins = mm(ps_u[0:CX, 0:XR], v_lo[:, s, t, :], p_hi[u % 3][0:KT, k, :],
                         start=False, stop=(t == NT - 1), skip_group_check=True)
                if k:
                    ins.then_inc(pv_done, 1)

            def side_work(i, step, name):
                wait(pe, side_free, side_count(i, step))
                if name == "S0q":
                    pe.wait_ge(xt_ld, 16 * (i + 3))
                    if isinstance(i, int) and i == -2:
                        pe.wait_ge(pads_set, 6)
                    for j in range(SJ):
                        ins = mm(side[:, j * PT:(j + 1) * PT], wq_pad[:, j, :, :].rearrange("c g r -> c (g r)"),
                                 xt[:, :], start=True, stop=True)
                elif name == "S0k":
                    mm(side[:, 0:PT], wk_pad[:, :, :].rearrange("c g r -> c (g r)"), xt[:, :], start=True, stop=True)
                    ins = mm(side[0:PT, 128:128 + SG * SD], xt[:, :],
                             swkv[:, 1, :, :].rearrange("c g d -> c (g d)"), start=True, stop=True)
                elif name == "S1":
                    g = S1_GROUP[step]
                    if isinstance(i, int) and i == -2 and g == 0:
                        pe.wait_ge(masks_set, 3)
                    mm(side[0:PT, 0:SJ * PT], ident_b[0:PT, :], mask_b[:, 0, :, :].rearrange("p j n -> p (j n)"),
                       start=True, stop=False, skip_group_check=True)
                    for j in range(SJ):
                        ins = mm(side[0:PT, j * PT:(j + 1) * PT], q_s[32 * g:32 * g + 32, j * PT:(j + 1) * PT],
                                 k_s[32 * g:32 * g + 32, :], start=False, stop=(j == SJ - 1), skip_group_check=True)
                elif name == "S2":
                    for j in range(SJ):
                        ins = mm(side[:, j * PT:(j + 1) * PT], m_pl[0:PT, j, :], ident[0:PT, 0:PT],
                                 start=True, stop=True)
                elif name == "S3":
                    g = S3_GROUP[step]
                    mm(side[0:PT, 0:SJ * PT], ident_b[0:PT, :], mask_b[:, 1, :, :].rearrange("p j n -> p (j n)"),
                       start=True, stop=False, skip_group_check=True)
                    ins = mm(side[0:PT, 0:SJ * PT], k_s[32 * g:32 * g + 32, :], q_m[32 * g:32 * g + 32, :],
                             start=False, stop=True, skip_group_check=True)
                elif name == "S4":
                    for h in range(SH):
                        g, j = h // SJ, h % SJ
                        ins = mm(side[0:PT, h * (SD + 1):(h + 1) * (SD + 1)], p_s[0:PT, g, j * PT:(j + 1) * PT],
                                 v_s[:, g, :], start=True, stop=True)
                elif name == "S5":
                    ins = nc.tensor.transpose(side[:, 0:PT], o_s[:, :], ident[0:PT, 0:PT])
                elif name == "S6":
                    if isinstance(i, int) and i == -1:
                        pe.wait_ge(swp_ld, 16)
                    ins = mm(side[0:PT, 0:C], o_t[:, :], swp[:, :], start=True, stop=True)
                elif name == "S7":
                    pe.wait_ge(x1_set, i + 2)
                    ins = nc.tensor.transpose(side[:, 0:PT], x1[:, :], ident[0:PT, 0:PT])
                elif name == "S8":
                    s = step // 12
                    if isinstance(i, int) and i == -1 and s == 0:
                        pe.wait_ge(qk_set, 1)
                    for h in range(XH):
                        ins = mm(side[0:CX, h * T:(h + 1) * T], qk_prod[:, h, :], x1t[:, s * T:(s + 1) * T],
                                 start=True, stop=True)
                elif name == "mrow":
                    pe.wait_ge(negm_set, 2 * i + step // 12 + 2)
                    for r in range(4):
                        ins = mm(side[CX:CX + 1, r * PT:(r + 1) * PT], negm[:, r:r + 1], ident[0:PT, 0:PT],
                                 start=True, stop=True)
                elif name[0] == "Y":
                    if step == 5:
                        pe.wait_ge(u_set, 2 * i)
                    for k, h in enumerate(Y_HEADS[step]):
                        ins = mm(side[0:PT, k * (C + 1):(k + 1) * (C + 1)], u_s[0:CX + 1, h, :], vo_prod[:, h, :],
                                 start=True, stop=True)
                elif name == "X2T":
                    pe.wait_ge(x2_set, i)
                    ins = nc.tensor.transpose(side[:, 0:PT], x2[:, :], ident[0:PT, 0:PT])
                ins.then_inc(side_full, 1)

            def k_seq(n):
                return seq_parity[0]

            seq_parity = [0]

            def body(i):
                here = parts(i)
                for step in range(24):
                    s, t = step // 12, step % 12
                    if "main" in here:
                        scores(i, s, t)
                    for at, name, part in SIDE:
                        if at == step and part in here:
                            side_work(i, step, name)
                    if ("second" if s else "main") in here:
                        seq_parity[0] = 1 - s
                        for k in MAXIMA.get(t, ()):
                            maxima(2 * i + s + 1, k)
                    if step < 4 and "post" in here:
                        sums(2 * i - 1, 1, 4 + t // 2, t % 2)
                    elif step >= 4 and "main" in here:
                        v = step - 4
                        sums(2 * i + v // 12, v // 12, v % 12 // 2, v % 2)

            iterate(pe, body, -2, LOOP_FROM, LOOP_TO, PAIRS + 1)

            pe.wait_ge(side_free, SIDE_END)
            pe.wait_ge(gw_lo_set, 1)
            for c in range(NB):
                wait(pe, lg_set, c - 1)
                if c == 0:
                    pe.wait_ge(a_max, 12 * B)
                dst, cols = ps_a[c % 2][0:EX, 0:FB], slice(c * FB, (c + 1) * FB)
                mm(dst, gw_hl[0][:, :], x2t[0][:, cols], start=True, stop=False)
                mm(dst, gw_hl[0][:, :], x2t[1][:, cols], start=False, stop=False)
                mm(dst, gw_hl[1][:, :], x2t[0][:, cols], start=False, stop=True).then_inc(lg_full, 1)
                pe.wait_ge(lg_set, c + 1)
                for q in range(PPB):
                    ins = nc.tensor.transpose(side[0:PT, (c * PPB + q) * EX:(c * PPB + q + 1) * EX],
                                              lg_t[:, c % 2, q * PT:(q + 1) * PT], ident[0:EX, 0:EX])
            ins.then_inc(side_full, 1)

            w_bank = ps_b[1][:, 0, :]
            fin_bank = ps_b[1][0:PT, 1, :]

            def weights_t():
                pe.wait_ge(gate_step, GATE_STEPS)
                for c in range(NB):
                    wait(pe, wt_set, c)
                    for q in range(PPB):
                        ins = nc.tensor.transpose(w_bank[0:2 * EX, q * PT:(q + 1) * PT], w_hl[:, c * PPB + q, :],
                                                  ident[0:PT, 0:PT])
                    ins.then_inc(wt_full, 1)
                pe.wait_ge(wt_set, NB)

            def expert(c, q):
                e, half = EXPERTS[q // 2], q % 2
                main, late = exists(c, NB), (exists(c, NB) if q >= 3 else exists(c, NB + 1, 1))
                n = UNITS * c + q
                if main:
                    if isinstance(c, int) and c == 0 and q == 2:
                        weights_t()
                    cols = slice((2 * e + half) * 128, (2 * e + half + 1) * 128)
                    moving = [part[:, bass.ds(c * FB, FB)] for part in x2t]
                    if e < EX and half == 0:
                        wait(pe, wb_set, EX * c + e)
                    for dst, w, used, full in ((ps_a[q % 2], wsp[0], silu_set, g_full),
                                               (ps_b[0][:, q % 2, :], wsp[1], hid_set, up_full)):
                        wait(pe, used, n - 1)
                        dst = dst[:, 0:FB]
                        mm(dst, w[0][:, cols], moving[0], start=True, stop=False)
                        mm(dst, w[0][:, cols], moving[1], start=False, stop=False)
                        mm(dst, w[1][:, cols], moving[0], start=False, stop=True).then_inc(full, 1)
                        if w is wsp[0] and e < EX and half == 0:
                            mm(w_bank[:, 0:FB], sel[:, e, :], wt_hl[:, bass.ds(c * FB, FB)],
                               start=True, stop=True).then_inc(wb_full, 1)
                if late:
                    r = (q - 3) % UNITS
                    e, half = EXPERTS[r // 2], r % 2
                    cols = slice((2 * e + half) * 128, (2 * e + half + 1) * 128)
                    pe.wait_ge(hid_lo_set, n - 2)
                    if r == 0:
                        wait(pe, y_set, c)
                    h_hi, h_lo = p_hi[r % 3][:, 0, :], p_lo[r % 3][:, 0, :]
                    dst = ps_u[:, 0:FB]
                    mm(dst, wsp[2][0][:, cols], h_hi, start=(r == 0), stop=False, skip_group_check=True)
                    mm(dst, wsp[2][0][:, cols], h_lo, start=False, stop=False, skip_group_check=True)
                    mm(dst, wsp[2][1][:, cols], h_hi, start=False, stop=(r == UNITS - 1), skip_group_check=True)\
                        .then_inc(down_done, 1)
                if q == 4 and exists(c, NB + 1, 1):
                    pe.wait_ge(y_set, c)
                    wait(pe, fin_set, c - 1)
                    for k in range(PPB):
                        ins = nc.tensor.transpose(fin_bank[:, k * C:(k + 1) * C], y_t[:, k * PT:(k + 1) * PT], ident)
                    ins.then_inc(fin_full, 1)

            def experts(c):
                for q in range(UNITS if exists(c, NB) else 8):
                    expert(c, q)

            iterate(pe, experts, 0, 2, NB, NB + 1)

        @block.scalar
        def _(act):
            act_f = nc.scalar.activation

            def copy(dst, src):
                return act_f(dst, src, ACT.Copy)

            act.wait_ge(prod_full, 1)
            copy(qk_prod[:, :, :].rearrange("p (a h) c -> p a (h c)", a=2), ps_b[0][:, :, 0:4 * CX]).then_inc(qk_set, 1)
            act.wait_ge(gw_ld, 16)
            copy(gw_hl[0][:, :], gw[:, :]).then_inc(gw_hi_set, 1)

            def split_weights(n):
                act.wait_ge(w_ld, 16 * (n + 1))
                copy(wsp[n][0][:, :], x_all[:, :]).then_inc(w_hi_set, 1)

            def exp_first(n, u):
                act.wait_ge(b_full, 6 * n + u + 1)
                wait(act, pv_done, 6 * n + u - 2)
                act_f(p_hi[u % 3][0:KT, :, :], ps_b[u % 2][0:KT, :, 0:XR], ACT.Exp, scale=X_SCALE).then_inc(exp_hi, 1)

            def exp_second(n, u):
                act.wait_ge(exp_hi, 6 * n + u + 1)
                b = ps_b[u % 2][0:KT, :, 0:XR]
                act_f(b, b, ACT.Exp, scale=X_SCALE).then_inc(exp_raw, 1)

            def side_work(i, step, name):
                if name in ("S4", "S6", "S1", "S2") or name[0] == "Y":
                    return
                act.wait_ge(side_full, side_count(i, step) + 1)
                if name == "S0q":
                    copy(q_hi[:, :], side[:, 0:SJ * PT]).then_inc(q_hi_set, 1)
                elif name == "S0k":
                    act_f(k_hi[:, :], side[:, 0:PT], ACT.Identity, bias=k_ones).then_inc(k_hi_set, 1)
                elif name == "S3":
                    act_f(p_s[0:PT, S3_GROUP[step], :], side[0:PT, 0:SJ * PT], ACT.Exp, scale=S_SCALE)\
                        .then_inc(side_free, 1)
                elif name == "S5":
                    copy(o_t[:, :], side[:, 0:PT]).then_inc(side_free, 1)
                elif name == "S7":
                    copy(x1t[:, :], side[:, 0:PT]).then_inc(side_free, 1)
                elif name == "S8":
                    n = 2 * i + 2 + step // 12
                    wait(act, a_full, 12 * n)
                    wait(act, qb_set, n)
                    copy(qa_hi[:, :], side[0:CX, 0:XR]).then_inc(qa_hi_set, 1)
                elif name == "mrow":
                    copy(qb_hi[CX:CX + 1, 1 - step // 12, :], side[CX:CX + 1, 0:XR]).then_inc(side_free, 1)
                elif name == "X2T":
                    copy(x2t[0][:, bass.ds((i - 1) * PT, PT)], side[:, 0:PT]).then_inc(x2t_hi_set, 1)

            def save_sums(n, s):
                act.wait_ge(pv_done, 6 * (n + 1))
                copy(u_s[0:CX + 1, :, s * T:(s + 1) * T],
                     ps_u[0:CX + 1, 0:XR].rearrange("p (h t) -> p h t", h=XH)).then_inc(u_set, 1)

            def body(i):
                here = parts(i)
                for step in range(24):
                    s, t = step // 12, step % 12
                    if isinstance(i, int) and (i, step) in SPLIT_STEPS:
                        split_weights(SPLIT_STEPS.index((i, step)))
                    if t % 2 and "main" in here:
                        exp_first(2 * i + s, t // 2)
                    if t % 2 == 0:
                        if step == 0 and "post" in here:
                            exp_second(2 * i - 1, 5)
                        elif step and "main" in here:
                            exp_second(2 * i + (step - 1) // 12, (t // 2 - 1) % 6)
                    if step == 4 and "post" in here:
                        save_sums(2 * i - 1, 1)
                    if step == 16 and "main" in here:
                        save_sums(2 * i, 0)
                    for at, name, part in SIDE:
                        if at == step and part in here:
                            side_work(i, step, name)

            iterate(act, body, -2, LOOP_FROM, LOOP_TO, PAIRS + 1)

            for c in range(NB):
                act.wait_ge(lg_full, c + 1)
                if c >= 2:
                    act.wait_ge(lg_full, c + 1)
                copy(lg_t[:, c % 2, :], ps_a[c % 2][0:EX, 0:FB]).then_inc(lg_set, 1)
            act.wait_ge(gate_step, 2)
            act_f(gt[:, 1, :, :], gt[:, 0, :, :], ACT.Exp).then_inc(gate_exp, 1)

            def expert(c, q):
                e, half = EXPERTS[q // 2], q % 2
                n = UNITS * c + q
                if exists(c, NB):
                    if isinstance(c, int) and c == 0 and q == 2:
                        for k in range(NB):
                            act.wait_ge(wt_full, k + 1)
                            copy(wt_hl[:, k * FB:(k + 1) * FB], ps_b[1][0:2 * EX, 0, 0:FB]).then_inc(wt_set, 1)
                    act.wait_ge(g_full, n + 1)
                    wait(act, hid_set, n - 1)
                    act_f(silu_s[:, q % 2, :], ps_a[q % 2][:, 0:FB], ACT.Silu).then_inc(silu_set, 1)
                    if e < EX and half == 0:
                        act.wait_ge(wb_full, EX * c + e + 1)
                        wait(act, weighted, 2 * (EX * c + e - 1))
                        copy(wgt_b[:, e % 2, :], ps_b[1][:, 0, 0:FB]).then_inc(wb_set, 1)
                if exists(c, NB) if q else exists(c, NB + 1, 1):
                    r = (q - 1) % UNITS
                    act.wait_ge(hid_set, n)
                    wait(act, down_done, n - 3)
                    copy(p_hi[r % 3][:, 0, :], hid[:, r % 2, :]).then_inc(hid_hi_set, 1)
                if q == 3 and exists(c, NB + 1, 1):
                    act.wait_ge(down_done, UNITS * c)
                    wait(act, fin_full, c - 1)
                    copy(y_t, ps_u[:, 0:FB]).then_inc(y_set, 1)

            def experts(c):
                for q in range(UNITS if exists(c, NB) else 8):
                    expert(c, q)

            iterate(act, experts, 0, 2, NB, NB + 1)

        @block.vector
        def _(dve):
            tt, ts, stt, cp = nc.vector.tensor_tensor, nc.vector.tensor_scalar, nc.vector.scalar_tensor_tensor, \
                nc.vector.tensor_copy
            dve.wait_ge(cst_ld, 16)
            cp(ident_b[:, :], ident[:, 0:PT]).then_inc(masks_set, 1)
            for m in range(2):
                cp(mask_b[:, m, :, :], over(cst[0:PT, None, 131 + m * PT:131 + (m + 1) * PT], [PT, SJ, PT]))\
                    .then_inc(masks_set, 1)
            row_fill = nc.vector.memset
            row_fill(vo_prod[CX:CX + 1, :, 0:C], 0.0).then_inc(rows_set, 1)
            row_fill(vo_prod[CX:CX + 1, :, C:C + 1], 1.0).then_inc(rows_set, 1)
            row_fill(bits(ct_hi[CX:CX + 1, :, :]), 1.0).then_inc(rows_set, 1)
            dve.wait_ge(sw_ld, 32)
            dve.wait_ge(zeroed, 8)
            for r in range(3):
                cp(wq_pad[:, :, :, r * SD:(r + 1) * SD],
                   swq[:, :, :, :].rearrange("c g j d -> c j g d")).then_inc(pads_set, 1)
                cp(wk_pad[:, :, r * SD:(r + 1) * SD], swkv[:, 0, :, :]).then_inc(pads_set, 1)
            dve.wait_ge(prod_full, 2)
            cp(vo_prod[0:CX, :, 0:C], ps_b[1][0:CX, :, :].rearrange("p a (h c) -> p (a h) c", h=4)).then_inc(vo_set, 1)
            dve.wait_ge(gw_hi_set, 1)
            tt(gw_hl[1][:, :], gw[:, :], bits(gw_hl[0][:, :]), ALU.subtract).then_inc(gw_lo_set, 1)

            def split_weights(n):
                dve.wait_ge(w_hi_set, n + 1)
                tt(wsp[n][1][:, :], x_all[:, :], bits(wsp[n][0][:, :]), ALU.subtract).then_inc(w_split, 1)

            def maxima(n, k):
                dve.wait_ge(a_full, 12 * n + k + 1)
                nc.vector.tensor_reduce(mx[:, k % 4, k // 4:k // 4 + 1], ps_a[k % 2][0:PT, 0:CHUNK], AX.X,
                                        ALU.max).then_inc(a_max, 1)
                if k == 11:
                    dve.wait_ge(a_max, 12 * (n + 1))
                    nc.vector.tensor_reduce(negm[:, :], mx[:, :, :], AX.X, ALU.max, negate=True).then_inc(negm_set, 1)

            def probs_lo(n, u):
                dve.wait_ge(exp_raw, 6 * n + u + 1)
                tt(p_lo[u % 3][0:KT, :, :], ps_b[u % 2][0:KT, :, 0:XR], bits(p_hi[u % 3][0:KT, :, :]),
                   ALU.subtract).then_inc(plo_set, 1)

            def side_work(i, step, name):
                use = side_count(i, step)
                if name in ("S3", "S5", "S7", "mrow"):
                    return
                if name not in ("S0q", "S0k", "S8", "X2T"):
                    dve.wait_ge(side_full, use + 1)
                if name == "S0q":
                    dve.wait_ge(q_hi_set, i + 3)
                    stt(q_s[:, :], bits(q_hi[:, :]), q_part, side[:, 0:SJ * PT], ALU.mult, ALU.add)\
                        .then_inc(side_free, 1)
                elif name == "S0k":
                    dve.wait_ge(k_hi_set, i + 3)
                    stt(k_s[:, :], bits(k_hi[:, :]), k_part, side[:, 0:PT], ALU.mult, ALU.add)
                    cp(v_s[:, :, 0:SD], side[0:PT, 128:128 + SG * SD].rearrange("p (g d) -> p g d", g=SG))\
                        .then_inc(side_free, 1)
                elif name == "S1":
                    at = 32 * S1_GROUP[step] + MAX_ROW
                    nc.vector.tensor_reduce(m_pl[0:PT, :, at:at + 1],
                                            side[0:PT, 0:SJ * PT].rearrange("p (j n) -> p j n", j=SJ), AX.X, ALU.max,
                                            negate=True).then_inc(side_free, 1)
                elif name == "S2":
                    tt(q_m[:, :], side[:, 0:SJ * PT], bits(q_s[:, :]), ALU.add).then_inc(side_free, 1)
                elif name == "S4":
                    o = side[0:PT, 0:SH * (SD + 1)].rearrange("p (h d) -> p h d", h=SH)
                    nc.vector.reciprocal(rl_s[:, :], side[0:PT, SD:SH * (SD + 1):SD + 1]).then_inc(rl_set, 1)
                    dve.wait_ge(rl_set, i + 2)
                    tt(o_s[:, :].rearrange("p (h d) -> p h d", h=SH), o[:, :, 0:SD],
                       over(rl_s[:, :, None], [PT, SH, SD]), ALU.mult).then_inc(side_free, 1)
                elif name == "S6":
                    dve.wait_ge(xr_set, i + 2)
                    tt(r1[:, :], side[0:PT, 0:C], xr[:, :], ALU.add).then_inc(side_free, 1)
                    dve.wait_ge(side_free, use + 1)
                    nc.vector.bn_stats(st1[:, :], r1[:, :]).then_inc(st1_set, 1)
                    dve.wait_ge(st1_set, i + 2)
                    take_wait(nc.vector)
                    nc.vector.bn_aggr(mv1[:, :], st1[:, :]).then_inc(mv1_set, 1)
                elif name == "S8":
                    dve.wait_ge(qa_hi_set, 2 * i + 3 + step // 12)
                    tt(qa_lo[:, :], side[0:CX, 0:XR], bits(qa_hi[:, :]), ALU.subtract).then_inc(side_free, 1)
                elif name[0] == "Y":
                    heads = Y_HEADS[step]
                    if step == 5:
                        dve.wait_ge(acc_init, i)
                    nc.vector.reciprocal(ry[:, 0:len(heads)], side[0:PT, C:len(heads) * (C + 1):C + 1])\
                        .then_inc(ry_set, 1)
                    dve.wait_ge(ry_set, 3 * (i - 1) + list(Y_HEADS).index(step) + 1)
                    for k, h in enumerate(heads):
                        ins = stt(acc[:, :], side[0:PT, k * (C + 1):k * (C + 1) + C], ry[:, k:k + 1], acc[:, :],
                                  ALU.mult, ALU.add)
                        if k < len(heads) - 1:
                            ins.then_inc(acc_set, 1)
                            dve.wait_ge(acc_set, 5 * (i - 1) + {5: 0, 7: 2, 11: 4}[step] + k + 1)
                    ins.then_inc(side_free, 1)
                    dve.wait_ge(side_free, use + 1)
                elif name == "X2T":
                    dve.wait_ge(x2t_hi_set, i)
                    cols = bass.ds((i - 1) * PT, PT)
                    tt(x2t[1][:, cols], side[:, 0:PT], bits(x2t[0][:, cols]), ALU.subtract).then_inc(side_free, 1)

            def body(i):
                here = parts(i)
                for step in range(24):
                    s, t = step // 12, step % 12
                    if isinstance(i, int) and (i, step) in SPLIT_STEPS:
                        split_weights(SPLIT_STEPS.index((i, step)))
                    for at, name, part in SIDE:
                        if at == step and part in here:
                            side_work(i, step, name)
                    if step == 7 and "second" in here:
                        dve.wait_ge(rstd1_set, i + 2)
                        wait(dve, xb_set, i + 1)
                        ts(x1[:, :], r1[:, :], mv1[:, 0:1], rstd1[:, 1:2], ALU.subtract, ALU.mult).then_inc(x1_set, 1)
                    if step == 12 and "post" in here:
                        nc.vector.bn_stats(st2[:, :], acc[:, :]).then_inc(st2_set, 1)
                        dve.wait_ge(st2_set, i)
                        take_wait(nc.vector)
                        nc.vector.bn_aggr(mv2[:, :], st2[:, :]).then_inc(mv2_set, 1)
                    if step == 14 and "post" in here:
                        dve.wait_ge(rstd2_set, i)
                        wait(dve, x2_kept, i - 1)
                        ts(x2[:, :], acc[:, :], mv2[:, 0:1], rstd2[:, 1:2], ALU.subtract, ALU.mult).then_inc(x2_set, 1)
                    if ("second" if s else "main") in here:
                        for k in MAXIMA.get(t, ()):
                            maxima(2 * i + s + 1, k)
                    if t % 2 == 0:
                        if step == 0 and "post" in here:
                            probs_lo(2 * i - 1, 5)
                        elif step and "main" in here:
                            probs_lo(2 * i + (step - 1) // 12, (t // 2 - 1) % 6)

            iterate(dve, body, -2, LOOP_FROM, LOOP_TO, PAIRS + 1)

            steps = [0]

            def step(ins):
                steps[0] += 1
                ins.then_inc(gate_step, 1)
                dve.wait_ge(gate_step, steps[0])

            tt(sel, over(ident[0:2 * EX, 0:EX, None], [2 * EX, EX, 128]),
               over(ident[0:2 * EX, EX:2 * EX, None], [2 * EX, EX, 128]), ALU.add).then_inc(sel_set, 1)
            dve.wait_ge(side_full, SIDE_END + 1)
            logits = side[0:PT, 0:PAIRS * EX].rearrange("p (q e) -> p q e", q=PAIRS)
            full = [PT, PAIRS, EX]
            step(nc.vector.tensor_reduce(g1[:, 0, :], logits, AX.X, ALU.max, negate=True))
            step(tt(gt[:, 0, :, :], logits, over(g1[:, 0, :, None], full), ALU.add))
            dve.wait_ge(gate_exp, 1)
            step(nc.vector.tensor_reduce(g1[:, 1, :], gt[:, 1, :, :], AX.X, ALU.add))
            step(nc.vector.reciprocal(g1[:, 2, :], g1[:, 1, :]))
            step(tt(gt[:, 2, :, :], gt[:, 1, :, :], over(g1[:, 2, :, None], full), ALU.mult))
            for q in range(PAIRS):
                ins = nc.vector.max(gt[:, 3, q, :], gt[:, 2, q, :])
            step(ins)
            for q in range(PAIRS):
                ins = nc.vector.max_index(gi[:, q, :], gt[:, 3, q, :], gt[:, 2, q, :])
            step(ins)
            step(cp(gt[:, 4, :, :], gi[:, :, :]))
            step(tt(g1[:, 3, :], gt[:, 3, :, 0], gt[:, 3, :, 1], ALU.add))
            step(ts(g1[:, 4, :], g1[:, 3, :], 1e-20, None, ALU.add))
            step(nc.vector.reciprocal(g1[:, 5, :], g1[:, 4, :]))
            for k in range(2):
                step(tt(g1[:, 6, :], gt[:, 3, :, k], g1[:, 5, :], ALU.mult))
                step(tt(gt[:, 5 + k, :, :], over(iota8[:, None, :], full), over(gt[:, 4, :, k:k + 1], full),
                        ALU.is_equal))
                step(tt(gt[:, 5 + k, :, :], gt[:, 5 + k, :, :], over(g1[:, 6, :, None], full), ALU.mult))
            step(tt(gt[:, 7, :, :], gt[:, 5, :, :], gt[:, 6, :, :], ALU.add))
            step(cp(w_h[:, :, :], gt[:, 7, :, :]))
            step(cp(w_hl[:, :, 0:EX], bits(w_h[:, :, :])))
            step(tt(w_hl[:, :, EX:2 * EX], gt[:, 7, :, :], bits(w_h[:, :, :]), ALU.subtract))
            assert steps[0] == GATE_STEPS

            def expert(c, q):
                e = EXPERTS[q // 2]
                n = UNITS * c + q
                if exists(c, NB):
                    if e < EX:
                        dve.wait_ge(weighted, 2 * EX * c + q - 1)
                    else:
                        dve.wait_ge(silu_set, n + 1)
                    dve.wait_ge(up_full, n + 1)
                    wait(dve, hid_lo_set, n - 1)
                    tt(hid[:, q % 2, :], silu_s[:, q % 2, :], ps_b[0][:, q % 2, 0:FB], ALU.mult).then_inc(hid_set, 1)
                if exists(c, NB) if q else exists(c, NB + 1, 1):
                    r = (q - 1) % UNITS
                    dve.wait_ge(hid_hi_set, n)
                    tt(p_lo[r % 3][:, 0, :], hid[:, r % 2, :], bits(p_hi[r % 3][:, 0, :]), ALU.subtract)\
                        .then_inc(hid_lo_set, 1)
                if q == 5 and exists(c, NB + 1, 1):
                    dve.wait_ge(fin_full, c)
                    tt(fin[:, :, :].rearrange("p q n -> p (q n)"), ps_b[1][0:PT, 1, :],
                       x_rows[:, bass.ds((c - 1) * PPB * C, PPB * C)], ALU.add).then_inc(fin_set, 1)
                    dve.wait_ge(fin_set, c)
                    for k in range(PPB):
                        ins = nc.vector.bn_stats(st3[:, k, :], fin[:, k, :])
                    ins.then_inc(st3_set, 1)
                    dve.wait_ge(st3_set, c)
                    take_wait(nc.vector)
                    for k in range(PPB):
                        ins = nc.vector.bn_aggr(mv3[:, k, :], st3[:, k, :])
                    ins.then_inc(mv3_set, 1)
                if q == 7 and exists(c, NB + 1, 1):
                    dve.wait_ge(rstd3_set, c)
                    wait(dve, out_st, 16 * (c - 1))
                    for k in range(PPB):
                        ts(out_s[:, k, :], fin[:, k, :], mv3[:, k, 0:1], rstd3[:, 1, k:k + 1],
                           ALU.subtract, ALU.mult).then_inc(out_set, 1)

            def experts(c):
                for q in range(UNITS if exists(c, NB) else 8):
                    expert(c, q)

            iterate(dve, experts, 0, 2, NB, NB + 1)

        @block.gpsimd
        def _(pool):
            ptt, pcp, fill = nc.gpsimd.tensor_tensor, nc.gpsimd.tensor_copy, nc.gpsimd.memset
            for ap, value in ((wq_pad[:, :, :, :], 0.0), (wk_pad[:, :, :], 0.0), (m_pl[:, :, :], 0.0),
                              (v_s[:, :, :], 1.0), (eps[:, :], EPS), (nhalf[:, :], -0.5),
                              (vo_prod[0:CX, :, C:C + 1], 0.0), (bits(v_hi[:, :, :, CX:CX + 1]), 1.0)):
                fill(ap, value).then_inc(zeroed, 1)
            pool.wait_ge(zeroed, 8)

            def split_ct(n, s, c):
                cols = slice(c * CHUNK, (c + 1) * CHUNK)
                pool.wait_ge(ct_ld[c], 16 * (n + 1))
                wait(pool, b_full, 6 * (n - 2) + 2 * c + 2)
                take_wait(nc.gpsimd)
                pcp(ct_hi[0:CX, s, cols], ct_raw[0:CX, c, :]).then_inc(cthi_set, 1)
                pool.wait_ge(cthi_set, 3 * n + c + 1)
                ptt(ct_lo[:, s, cols], ct_raw[0:CX, c, :], bits(ct_hi[0:CX, s, cols]), ALU.subtract)\
                    .then_inc(ctlo_set, 1)

            def split_v(n, s, part):
                tiles = slice(part * 4, part * 4 + 4)
                if part == 0:
                    pool.wait_ge(v_ld, 16 * (n + 1))
                    wait(pool, pv_done, 6 * (n - 1))
                take_wait(nc.gpsimd)
                pcp(v_hi[:, s, tiles, 0:CX], v_raw_t[:, tiles, :]).then_inc(vhi_set, 1)
                pool.wait_ge(vhi_set, 3 * n + part + 1)
                ins = ptt(v_lo[:, s, tiles, :], v_raw_t[:, tiles, :], bits(v_hi[:, s, tiles, 0:CX]), ALU.subtract)
                if part == 2:
                    ins.then_inc(vlo_set, 1)

            def rstd(out2, var, n, ve_set, done):
                width = out2[0].shape[-1]
                ptt(out2[0], var, eps[0:PT, 0:width], ALU.add).then_inc(ve_set, 1)
                pool.wait_ge(ve_set, n)
                ptt(out2[1], out2[0], nhalf[0:PT, 0:width], ALU.pow).then_inc(done, 1)

            def body(i):
                here = parts(i)
                for step in range(0 if isinstance(i, int) and i == -2 else 24):
                    s, t = step // 12, step % 12
                    n = 2 * i + s
                    if t == 0 and exists(n + 1):
                        split_ct(n + 1, 1 - s, 2)
                    if t in (4, 8) and exists(n + 2):
                        split_ct(n + 2, s, t // 4 - 1)
                    if t in (5, 7, 10) and exists(n + 1):
                        split_v(n + 1, 1 - s, (5, 7, 10).index(t))
                    if t == 2 and exists(n + 1):
                        pool.wait_ge(side_free, (side_count(i, 10) if s else side_count_before(i, 22)) + 1)
                        wait(pool, b_full, 6 * n)
                        take_wait(nc.gpsimd)
                        pcp(qb_hi[0:CX, 1 - s, :], bits(qa_hi[:, :]))
                        pcp(qb_lo[:, 1 - s, :], bits(qa_lo[:, :])).then_inc(qb_set, 1)
                    if step == 3 and "second" in here:
                        if isinstance(i, int) and i == -1:
                            pool.wait_ge(bias_ld, 16)
                        pool.wait_ge(xn_ld, 16 * (i + 2))
                        wait(pool, mv1_set, i + 1)
                        ptt(xr[:, :], xn[:, :], bias2[:, 0, :], ALU.add).then_inc(xr_set, 1)
                    if step == 5 and "post" in here:
                        wait(pool, x2_set, i - 1)
                        pool.wait_ge(xb_set, i)
                        take_wait(nc.gpsimd)
                        pcp(acc[:, :], x_rows[:, bass.ds((i - 1) * C, C)]).then_inc(acc_init, 1)
                    if step == 6 and "second" in here:
                        pool.wait_ge(mv1_set, i + 2)
                        rstd((rstd1[:, 0:1], rstd1[:, 1:2]), mv1[:, 1:2], i + 2, ve1_set, rstd1_set)
                    if step == 9 and "second" in here:
                        if isinstance(i, int) and i == -1:
                            pool.wait_ge(w_split, 3)
                        pool.wait_ge(x1_set, i + 2)
                        ptt(x_rows[:, bass.ds((i + 1) * C, C)], x1[:, :], bias2[:, 1, :], ALU.add).then_inc(xb_set, 1)
                    if step == 13 and "post" in here:
                        pool.wait_ge(mv2_set, i)
                        rstd((rstd2[:, 0:1], rstd2[:, 1:2]), mv2[:, 1:2], i, ve2_set, rstd2_set)
                    if step == 15 and "post" in here:
                        pool.wait_ge(x2_set, i)
                        take_wait(nc.gpsimd)
                        pcp(x_rows[:, bass.ds((i - 1) * C, C)], x2[:, :]).then_inc(x2_kept, 1)

            iterate(pool, body, -2, LOOP_FROM, LOOP_TO, PAIRS + 1)

            def expert(c, q):
                e, half = EXPERTS[q // 2], q % 2
                if exists(c, NB) and e < EX:
                    pool.wait_ge(silu_set, UNITS * c + q + 1)
                    pool.wait_ge(wb_set, EX * c + e + 1)
                    ptt(silu_s[:, q % 2, :], silu_s[:, q % 2, :], wgt_b[:, e % 2, :], ALU.mult).then_inc(weighted, 1)
                if q == 6 and exists(c, NB + 1, 1):
                    pool.wait_ge(mv3_set, c)
                    rstd((rstd3[:, 0, :], rstd3[:, 1, :]), mv3[:, :, 1], c, ve3_set, rstd3_set)

            def experts(c):
                for q in range(UNITS if exists(c, NB) else 8):
                    expert(c, q)

            iterate(pool, experts, 0, 2, NB, NB + 1)


def constants():
    cst = np.zeros((128, CONST_COLS), np.float32)
    cst[:, 0:128] = np.eye(128)
    row = np.arange(128) % 32
    cst[:, 128] = np.where((row >= SD) & (row < 2 * SD), -1.0, 0.0)
    cst[:, 129] = np.where((row >= 2 * SD) & (row < 3 * SD), -1.0, 0.0)
    cst[:, 129] += np.where(row == MAX_ROW, 1.0, 0.0)
    cst[:, 130] = np.where(row == MAX_ROW, 1.0, 0.0)
    q, k = np.arange(PT)[:, None], np.arange(PT)[None, :]
    mask = np.where((q // T == k // T) & (k <= q), 0.0, MASKED)
    cst[0:PT, 131:131 + PT] = mask
    cst[0:PT, 131 + PT:131 + 2 * PT] = mask.T
    cst[:, 131 + 2 * PT:] = np.arange(EX)
    return cst


def kernel(**inputs):
    import concourse.bacc as bacc
    from concourse.bass_utils import run_bass_kernel_spmd

    a = {n: np.asarray(v) for n, v in inputs.items()}
    x = a["x"].reshape(B * T, C)
    context = a["ctx_768"].reshape(B, KT, NT, CX)
    shared = {n: a["L0_ffn_ws_" + n] for n in ("gate", "up", "down")}
    wide = {n: np.concatenate([a["L0_ffn_w_" + n], shared[n][None]]).transpose(1, 0, 2).reshape(C, -1)
            for n in ("gate", "up")}
    down = np.concatenate([a["L0_ffn_w_down"], shared["down"][None]]).reshape(EX + 1, 2, 128, C)
    s_bias = np.concatenate([a["L0_attn_bp"], a["L0_xattn_bo"]])
    arrays = {
        "x_t": x.T, "x_n": x,
        "ctx_n": context.reshape(B * KT, NT * CX),
        "ctx_t": context.transpose(0, 3, 2, 1).reshape(B * CX, KV),
        "s_wq_t": a["L0_attn_Wq"].reshape(SH * SD, C).T,
        "s_wkv_t": np.concatenate([a["L0_attn_Wk"].reshape(SG * SD, C), a["L0_attn_Wv"].reshape(SG * SD, C)]).T,
        "s_wp_t": a["L0_attn_Wp"].T,
        "s_bias": np.broadcast_to(s_bias, (PT, 2 * C)),
        "x_wq_t": a["L0_xattn_Wq"].T, "x_wk_t": a["L0_xattn_Wk"].T, "x_wv_t": a["L0_xattn_Wv"].T,
        "x_wo": a["L0_xattn_Wo"],
        "gate_w": a["L0_ffn_gate_w"], "w_gate": wide["gate"], "w_up": wide["up"],
        "w_down": down.transpose(2, 0, 1, 3).reshape(128, -1),
        "consts": constants(),
    }
    nc = bacc.Bacc("TRN2", target_bir_lowering=False, num_devices=1)
    feeds, args = {}, []
    for name, value in arrays.items():
        value = np.ascontiguousarray(value)
        feeds["in_" + name] = value
        args.append(nc.dram_tensor("in_" + name, value.shape, mybir.dt.from_np(value.dtype), kind="ExternalInput").ap())
    out = nc.dram_tensor("out", (B * T, C), F32, kind="ExternalOutput").ap()
    bass_decoder_layer(nc, *args, out)
    result = run_bass_kernel_spmd(nc, [feeds], core_ids=[0])
    return result.results[0]["out"].reshape(B, T, C)
```

```python
from contextlib import ExitStack

import numpy as np
import concourse.bass as bass
from concourse import mybir

ALU = mybir.AluOpType
ACT = mybir.ActivationFunctionType
F32 = mybir.dt.float32
F32R = mybir.dt.float32r
BF16 = mybir.dt.bfloat16
U32 = mybir.dt.uint32
AX = mybir.AxisListType

B, T, C = 32, 56, 128
PT = 2 * T
PAIRS = B // 2
KV, CX = 1500, 96
KT, NT = 125, 12
CHUNK = 4 * KT
XH, XD = 8, 64
XR = XH * T
SH, SG, SJ, SD = 16, 4, 4, 8
EX, ED = 8, 256
FB = 448
NB = B * T // FB
PPB = FB // PT
EPS = 1e-5
S_SCALE = SD ** -0.5
X_SCALE = XD ** -0.5
MASKED = -1e30
MAX_ROW = 24

SIDE = [(0, "S8", "main"), (1, "S3", "second"), (2, "S3", "second"), (3, "S4", "second"),
        (5, "Y0", "post"), (6, "S5", "second"), (7, "Y1", "post"), (8, "S6", "second"),
        (9, "Y2", "post"), (10, "mrow", "main"), (11, "S7", "second"), (12, "S8", "second"),
        (13, "S0q", "first"), (14, "S0k", "first"), (15, "S1", "first"), (16, "S1", "first"),
        (17, "S1", "first"), (18, "S1", "first"), (19, "X2T", "post"), (20, "S2", "first"),
        (21, "S3", "first"), (22, "mrow", "second"), (23, "S3", "first")]
S0K_STEP = 14
S1_GROUP = {15: 0, 16: 1, 17: 2, 18: 3}
S3_GROUP = {21: 0, 23: 1, 1: 2, 2: 3}
Y_HEADS = {5: (0, 1, 2), 7: (3, 4, 5), 9: (6, 7)}
MAXIMA = {1: (0, 1), 2: (2, 3), 3: (4, 5), 4: (6,), 5: (7, 8), 6: (9,), 7: (10, 11),
          13: (0, 1), 14: (2,), 15: (3,), 16: (4,), 17: (5, 6), 18: (7,), 19: (8, 9), 20: (10, 11)}
SIDE_FIRST = (0, 8, 10, 12, 14, 20)
LOOP_FROM, LOOP_TO = 2, PAIRS - 2


def parts(i):
    if not isinstance(i, int):
        return {"main", "post", "second", "first"}
    return {name for name, lo, hi in (("main", 0, PAIRS), ("post", 1, PAIRS + 1),
                                      ("second", -1, PAIRS - 1), ("first", -2, PAIRS - 2))
            if lo <= i < hi}


def side_count(i, step):
    here = sum(1 for s, _, part in SIDE if s < step and part in parts(i))
    if not isinstance(i, int):
        return len(SIDE) * i + (side_count(LOOP_FROM, 0) - len(SIDE) * LOOP_FROM + here)
    return here + sum(1 for j in range(-2, i) for _, _, part in SIDE if part in parts(j))


def side_count_before(i, step):
    if isinstance(i, int):
        return side_count(i - 1, step)
    return side_count(i, 0) - sum(1 for s, _, _ in SIDE if s >= step)


SIDE_END = side_count(PAIRS + 1, 0)
EW = (EX + 1) * ED
W_STEP = 11
W_PIECE = 3 * EW // PAIRS
EXPERTS = (EX,) + tuple(range(EX))
UNITS = 2 * len(EXPERTS)
GATE_STEPS = 21
CONST_COLS = 128 + 3 + 2 * PT + EX


def bass_decoder_layer(nc, x_t, x_n, ctx_n, ctx_t, s_wq_t, s_wkv_t, s_wp_t, s_bias, x_wq_t, x_wk_t, x_wv_t,
                       x_wo, gate_w, w_all, consts, out):
    with ExitStack() as ctx:
        def sb(name, shape, dt=F32):
            return ctx.enter_context(nc.sbuf_tensor(name, shape, dt))

        def ps(name, shape):
            return ctx.enter_context(nc.psum_tensor(name, shape, F32))

        def sem(name):
            return ctx.enter_context(nc.semaphore(name))

        cst = sb("cst", [128, CONST_COLS])
        ident = cst[:, 0:128]
        q_part, k_part, k_ones = (cst[:, 128 + n:129 + n] for n in range(3))
        iota8 = cst[0:PT, 131 + 2 * PT:139 + 2 * PT]
        ident_b = sb("ident_b", [128, PT], BF16)
        mask_b = sb("mask_b", [PT, 2, SJ, PT], BF16)
        eps = sb("eps", [128, 4])
        nhalf = sb("nhalf", [128, 4])
        spare = sb("spare", [128, 32])
        taken = [0]
        swq = sb("swq", [128, SG, SJ, SD])
        swkv = sb("swkv", [128, 2, SG, SD])
        swp = sb("swp", [128, C])
        bias2 = sb("bias2", [PT, 2, C])
        wq_pad = sb("wq_pad", [128, SJ, SG, 32])
        wk_pad = sb("wk_pad", [128, SG, 32])
        qk_prod = sb("qk_prod", [128, XH, CX])
        vo_prod = sb("vo_prod", [CX + 1, XH, C + 1])
        gw = sb("gw", [128, EX])
        gw_hl = [sb(f"gw_{p}", [128, EX], F32R) for p in ("hi", "lo")]
        w_hi = sb("w_hi", [128, 3 * EW], F32R)
        w_lo = sb("w_lo", [128, 3 * EW], F32R)
        w_raw = sb("w_raw", [128, W_PIECE])
        wsp = [[part[:, n * EW:(n + 1) * EW] for part in (w_hi, w_lo)] for n in range(3)]
        x_rows = sb("x_rows", [PT, PAIRS * C])
        x2t = [sb(f"x2t_{p}", [128, B * T], F32R) for p in ("hi", "lo")]
        xt = sb("xt", [128, PT])
        xn = sb("xn", [PT, C])
        xr = sb("xr", [PT, C])
        q_hi = sb("q_hi", [128, SJ * PT], F32R)
        q_s = sb("q_s", [128, SJ * PT], F32R)
        q_m = sb("q_m", [128, SJ * PT], F32R)
        k_hi = sb("k_hi", [128, PT], F32R)
        k_s = sb("k_s", [128, PT], F32R)
        v_s = sb("v_s", [PT, SG, SD + 1])
        m_pl = sb("m_pl", [128, SJ, 128])
        p_s = sb("p_s", [128, SG, SJ * PT])
        rl_s = sb("rl_s", [PT, SH])
        o_s = sb("o_s", [PT, C])
        o_t = sb("o_t", [C, PT])
        r1 = sb("r1", [PT, C])
        st1 = sb("st1", [PT, 6])
        mv1 = sb("mv1", [PT, 2])
        rstd1 = sb("rstd1", [PT, 2])
        x1 = sb("x1", [PT, C])
        x1t = sb("x1t", [C, PT])
        ct_raw = sb("ct_raw", [128, 3, CHUNK])
        ct_hi = sb("ct_hi", [CX + 1, 2, 3 * CHUNK], F32R)
        ct_lo = sb("ct_lo", [CX, 2, 3 * CHUNK], F32R)
        v_raw = sb("v_raw", [128, NT * CX])
        v_raw_t = v_raw[0:KT, :].rearrange("p (t c) -> p t c", t=NT)
        v_hi = sb("v_hi", [KT, 2, NT, CX + 1], F32R)
        v_lo = sb("v_lo", [KT, 2, NT, CX], F32R)
        xq_hi = sb("xq_hi", [CX + 1, 2, XR], F32R)
        xq_lo = sb("xq_lo", [CX, 2, XR], F32R)
        mx = sb("mx", [PT, 4, 3])
        negm = sb("negm", [PT, 4])
        p_hi = [sb(f"p_hi{n}", [128, 2, XR], F32R) for n in range(3)]
        p_lo = [sb(f"p_lo{n}", [128, 2, XR], F32R) for n in range(3)]
        u_s = sb("u_s", [128, XH, PT])
        ry = sb("ry", [PT, 4])
        y_h = sb("y_h", [PT, XH, C])
        acc = sb("acc", [PT, C])
        st2 = sb("st2", [PT, 6])
        mv2 = sb("mv2", [PT, 2])
        rstd2 = sb("rstd2", [PT, 2])
        x2 = sb("x2", [PT, C])
        ct_flat = ct_raw[:, :, :].rearrange("p c n -> p (c n)")
        u_flat = u_s[:, :, :].rearrange("p h n -> p (h n)")
        p_flat = p_s[0:PT, :, :].rearrange("p g n -> p (g n)")
        silu_s = ct_flat[:, 0:2 * FB].rearrange("p (k n) -> p k n", k=2)
        lg_t = silu_s[0:EX, :, :]
        hid = v_raw[:, 0:2 * FB].rearrange("p (k n) -> p k n", k=2)
        wgt_b = u_flat[:, 0:2 * FB].rearrange("p (k n) -> p k n", k=2)
        y_t = m_pl[:, :, :].rearrange("p j n -> p (j n)")[:, 0:FB]
        wt_hl = ct_hi[0:2 * EX, :, :].rearrange("p c n -> p (c n)")[:, 0:B * T]
        sel = ct_lo[0:2 * EX, :, :].rearrange("p c n -> p (c n)")[:, 0:EX * 128].rearrange("p (e m) -> p e m", e=EX)
        gt = p_flat[:, 0:8 * PAIRS * EX].rearrange("p (k q e) -> p k q e", k=8, e=EX)
        w_hl = p_flat[:, 8 * PAIRS * EX:10 * PAIRS * EX].rearrange("p (q e) -> p q e", q=PAIRS)
        g1 = sb("g1", [PT, 7, PAIRS])
        gi = sb("gi", [PT, PAIRS, 8], U32)
        w_h = sb("w_h", [PT, PAIRS, EX], F32R)
        fin = sb("fin", [PT, PPB, C])
        out_s = sb("out_s", [PT, PPB, C])
        st3 = sb("st3", [PT, PPB, 6])
        mv3 = sb("mv3", [PT, PPB, 2])
        rstd3 = sb("rstd3", [PT, 2, PPB])
        wq_f = p_s[0:XD, :, :].rearrange("p g n -> p (g n)")[:, 0:XH * C].rearrange("p (h c) -> p h c", h=XH)
        wk_f = p_s[0:XD, :, :].rearrange("p g n -> p (g n)")[:, XH * C:XH * (C + CX)].rearrange("p (h c) -> p h c", h=XH)
        wv_f = u_flat[0:XD, 0:XH * CX].rearrange("p (h c) -> p h c", h=XH)
        wo_f = v_raw[0:XD, 0:XH * C].rearrange("p (h c) -> p h c", h=XH)

        ps_a = [ps(f"ps_a{n}", [128, 512]) for n in range(2)]
        ps_b = [ps(f"ps_b{n}", [128, 2, 512]) for n in range(2)]
        ps_u = ps("ps_u", [128, 512])
        side_ps = ps("side", [128, 512])

        cst_ld, sw_ld, xw_ld, swp_ld, bias_ld, gw_ld, w_ld, xt_ld, xn_ld, v_ld, out_st = (sem(n) for n in (
            "cst_ld", "sw_ld", "xw_ld", "swp_ld", "bias_ld", "gw_ld", "w_ld", "xt_ld", "xn_ld", "v_ld", "out_st"))
        ct_ld = [sem(f"ct_ld{c}") for c in range(3)]
        zeroed, pads_set, masks_set, prod_full, qk_set, vo_set, w_hi_set, w_split = (sem(n) for n in (
            "zeroed", "pads_set", "masks_set", "prod_full", "qk_set", "vo_set", "w_hi_set", "w_split"))
        side_full, side_free = sem("side_full"), sem("side_free")
        rows_set = sem("rows_set")
        a_full, a_max, b_full, pv_done = (sem(n) for n in ("a_full", "a_max", "b_full", "pv_done"))
        exp_hi, exp_raw, plo_set = (sem(n) for n in ("exp_hi", "exp_raw", "plo_set"))
        negm_set, xq_hi_set, u_set = (sem(n) for n in ("negm_set", "xq_hi_set", "u_set"))
        cthi_set, ctlo_set, vhi_set, vlo_set = (sem(n) for n in ("cthi_set", "ctlo_set", "vhi_set", "vlo_set"))
        q_hi_set, k_hi_set, rl_set, st1_set, mv1_set, ve1_set, rstd1_set, x1_set, xr_set, xb_set = (sem(n) for n in (
            "q_hi_set", "k_hi_set", "rl_set", "st1_set", "mv1_set", "ve1_set", "rstd1_set", "x1_set", "xr_set", "xb_set"))
        ry_set, y_summed, st2_set, mv2_set, ve2_set, rstd2_set, x2_set, x2_kept, x2t_hi_set = (
            sem(n) for n in ("ry_set", "y_summed", "st2_set", "mv2_set", "ve2_set", "rstd2_set", "x2_set",
                             "x2_kept", "x2t_hi_set"))
        gw_hi_set, gw_lo_set, sel_set, lg_full, lg_set, gate_step, gate_exp, wt_full, wt_set = (sem(n) for n in (
            "gw_hi_set", "gw_lo_set", "sel_set", "lg_full", "lg_set", "gate_step", "gate_exp", "wt_full", "wt_set"))
        g_full, up_full, wb_full, wb_set, silu_set, weighted, hid_set, hid_hi_set, hid_lo_set, down_done = (
            sem(n) for n in ("g_full", "up_full", "wb_full", "wb_set", "silu_set", "weighted", "hid_set", "hid_hi_set",
                             "hid_lo_set", "down_done"))
        y_set, fin_full, fin_set, st3_set, mv3_set, ve3_set, rstd3_set, out_set = (sem(n) for n in (
            "y_set", "fin_full", "fin_set", "st3_set", "mv3_set", "ve3_set", "rstd3_set", "out_set"))

        def bits(ap):
            return ap.bitcast(F32)

        def over(ap, shape):
            return ap.broadcast_to(shape)

        def iterate(eng, body, first, loop_from, loop_to, last):
            for i in range(first, loop_from):
                body(i)
            with eng.Fori(loop_from, loop_to) as i:
                body(i)
            for i in range(loop_to, last):
                body(i)

        def alternates(i, step):
            return isinstance(i, int) and (i == -2 or (i == -1 and step < 22))

        def side_bank(i, step, group):
            return ps_u if alternates(i, step) and group % 2 else side_ps

        def exists(n, count=B, first=0):
            return not isinstance(n, int) or first <= n < count

        def wait(eng, s, n):
            if not isinstance(n, int) or n > 0:
                eng.wait_ge(s, n)

        def take_wait(eng):
            if eng is nc.vector:
                nc.vector.memset(spare[:, 0:1], 0.0)
            else:
                taken[0] = taken[0] % 31 + 1
                nc.gpsimd.tensor_tensor(spare[:, taken[0]:taken[0] + 1], eps[:, 0:1], eps[:, 0:1], ALU.add)

        block = ctx.enter_context(nc.Block())

        @block.sync
        def _(sp):
            sp.dma_start(swq[:, :, :, :], s_wq_t.rearrange("c (g j d) -> c g j d", g=SG, j=SJ)).then_inc(sw_ld, 16)
            sp.dma_start(swkv[:, :, :, :], s_wkv_t.rearrange("c (n g d) -> c n g d", n=2, g=SG)).then_inc(sw_ld, 16)
            sp.dma_start(xt[:, :], x_t[:, 0:PT]).then_inc(xt_ld, 16)
            sp.dma_start(cst[:, :], consts).then_inc(cst_ld, 16)
            for dst, src in ((wq_f, x_wq_t), (wk_f, x_wk_t), (wv_f, x_wv_t), (wo_f, x_wo)):
                sp.dma_start(dst, src.rearrange("(h d) c -> d h c", h=XH)).then_inc(xw_ld, 16)
            sp.dma_start(xn[:, :], x_n[0:PT, :]).then_inc(xn_ld, 16)
            sp.dma_start(swp[:, :], s_wp_t).then_inc(swp_ld, 16)
            sp.dma_start(bias2[:, :, :], s_bias.rearrange("p (n c) -> p n c", n=2)).then_inc(bias_ld, 16)
            for c in range(3):
                sp.dma_start(ct_raw[0:CX, c, :], ctx_t[0:CX, c * CHUNK:(c + 1) * CHUNK]).then_inc(ct_ld[c], 16)
            sp.dma_start(gw[:, :], gate_w).then_inc(gw_ld, 16)
            sp.dma_start(w_raw[:, :], w_all[:, 0:W_PIECE]).then_inc(w_ld, 16)
            sp.wait_ge(prod_full, 2)
            sp.dma_start(v_raw_t, ctx_n[0:KT, :].rearrange("p (t c) -> p t c", t=NT)).then_inc(v_ld, 16)

            def body(i):
                if isinstance(i, int) and i == -2:
                    sp.wait_ge(side_free, side_count(-2, S0K_STEP) + 1)
                    sp.dma_start(xt[:, :], x_t[:, PT:2 * PT]).then_inc(xt_ld, 16)
                    return
                for s in range(2):
                    n = 2 * i + s
                    if exists(n + 2, first=1):
                        wait(sp, ctlo_set, 3 * (n + 1) + 3)
                        sp.dma_start(ct_raw[0:CX, 2, :], ctx_t[bass.ds((n + 2) * CX, CX), 2 * CHUNK:3 * CHUNK])\
                          .then_inc(ct_ld[2], 16)
                    if s == 0 and exists(i + 2, PAIRS):
                        wait(sp, xr_set, i + 2)
                        sp.dma_start(xn[:, :], x_n[bass.ds((i + 2) * PT, PT), :]).then_inc(xn_ld, 16)
                    for c in range(2):
                        if exists(n + 3, first=1):
                            wait(sp, ctlo_set, 3 * (n + 2) + c + 1)
                            sp.dma_start(ct_raw[0:CX, c, :],
                                         ctx_t[bass.ds((n + 3) * CX, CX), c * CHUNK:(c + 1) * CHUNK])\
                              .then_inc(ct_ld[c], 16)
                        if c == 0 and exists(n + 2, first=1):
                            wait(sp, vlo_set, n + 2)
                            sp.dma_start(v_raw_t, ctx_n[bass.ds((n + 2) * KT, KT), :]
                                         .rearrange("p (t c) -> p t c", t=NT)).then_inc(v_ld, 16)
                    if s == 1 and exists(i + 1, PAIRS, 1):
                        sp.wait_ge(w_split, i + 1)
                        sp.dma_start(w_raw[:, :], w_all[:, bass.ds((i + 1) * W_PIECE, W_PIECE)]).then_inc(w_ld, 16)
                    if s == 1 and exists(i + 3, PAIRS):
                        sp.wait_ge(side_free, side_count(i, S0K_STEP) + 1)
                        sp.dma_start(xt[:, :], x_t[:, bass.ds((i + 3) * PT, PT)]).then_inc(xt_ld, 16)

            iterate(sp, body, -2, LOOP_FROM, PAIRS - 3, PAIRS)

            def store(c):
                sp.wait_ge(out_set, PPB * (c + 1))
                sp.dma_start(out[bass.ds(c * FB, FB), :].rearrange("(q p) n -> p q n", p=PT),
                             out_s[:, :, :]).then_inc(out_st, 16)

            iterate(sp, store, 0, 0, NB, NB)
            sp.wait_ge(out_st, 16 * NB)

        @block.tensor
        def _(pe):
            mm = nc.tensor.matmul

            def weight_product(dst, stationary, moving, width):
                for h in range(XH):
                    ins = mm(dst[:, h // 4, (h % 4) * width:(h % 4 + 1) * width], stationary[:, h, :], moving[:, h, :],
                             start=True, stop=True)
                ins.then_inc(prod_full, 1)

            def maxima(n, s, k):
                chunk, rows = k // 4, k % 4
                if k == 0:
                    pe.wait_ge(xq_hi_set, n + 1)
                if rows == 0:
                    pe.wait_ge(cthi_set, 3 * n + chunk + 1)
                wait(pe, a_max, 12 * n + k - 1)
                mm(ps_a[k % 2][0:PT, 0:CHUNK], xq_hi[0:CX, s, rows * PT:(rows + 1) * PT],
                   ct_hi[0:CX, s, chunk * CHUNK:(chunk + 1) * CHUNK], start=True, stop=True).then_inc(a_full, 1)

            def scores(i, s, t):
                n, u = 2 * i + s, t // 2
                if t == 0:
                    pe.wait_ge(side_free, (side_count(i, 10) if s else side_count_before(i, 22)) + 1)
                if t == 0 and isinstance(i, int) and i == 0 and s == 0:
                    pe.wait_ge(qk_set, 1)
                    pe.wait_ge(vo_set, 1)
                if t % 4 == 0:
                    pe.wait_ge(ctlo_set, 3 * n + t // 4 + 1)
                if t % 2 == 0:
                    wait(pe, plo_set, 6 * n + u - 1)
                dst = ps_b[u % 2][0:KT, t % 2, 0:XR]
                keys = slice(t * KT, (t + 1) * KT)
                mm(dst, ct_hi[:, s, keys], xq_hi[:, s, :], start=True, stop=False)
                mm(dst, ct_hi[0:CX, s, keys], xq_lo[:, s, :], start=False, stop=False)
                ins = mm(dst, ct_lo[:, s, keys], xq_hi[0:CX, s, :], start=False, stop=True)
                if t % 2:
                    ins.then_inc(b_full, 1)

            def sums(n, s, u, k):
                t = 2 * u + k
                if k == 0:
                    pe.wait_ge(plo_set, 6 * n + u + 1)
                if t == 0:
                    pe.wait_ge(vlo_set, n + 1)
                    wait(pe, u_set, n)
                mm(ps_u[0:CX + 1, 0:XR], v_hi[:, s, t, :], p_hi[u % 3][0:KT, k, :],
                   start=(t == 0), stop=False, skip_group_check=True)
                mm(ps_u[0:CX + 1, 0:XR], v_hi[:, s, t, :], p_lo[u % 3][0:KT, k, :],
                   start=False, stop=False, skip_group_check=True)
                ins = mm(ps_u[0:CX, 0:XR], v_lo[:, s, t, :], p_hi[u % 3][0:KT, k, :],
                         start=False, stop=(t == NT - 1), skip_group_check=True)
                if k:
                    ins.then_inc(pv_done, 1)

            def side_work(i, step, name):
                group = {"S1": S1_GROUP, "S3": S3_GROUP}.get(name, {}).get(step, 0)
                two_banks = alternates(i, step) and group > 0
                wait(pe, side_free, side_count(i, step) - (1 if two_banks else 0))
                side = side_bank(i, step, group)
                if name == "S0q":
                    pe.wait_ge(xt_ld, 16 * (i + 3))
                    if isinstance(i, int) and i == -2:
                        pe.wait_ge(pads_set, 6)
                    for j in range(SJ):
                        ins = mm(side[:, j * PT:(j + 1) * PT], wq_pad[:, j, :, :].rearrange("c g r -> c (g r)"),
                                 xt[:, :], start=True, stop=True)
                elif name == "S0k":
                    mm(side[:, 0:PT], wk_pad[:, :, :].rearrange("c g r -> c (g r)"), xt[:, :], start=True, stop=True)
                    ins = mm(side[0:PT, 128:128 + SG * SD], xt[:, :],
                             swkv[:, 1, :, :].rearrange("c g d -> c (g d)"), start=True, stop=True)
                elif name == "S1":
                    g = S1_GROUP[step]
                    if isinstance(i, int) and i == -2 and g == 0:
                        pe.wait_ge(masks_set, 3)
                    mm(side[0:PT, 0:SJ * PT], ident_b[0:PT, :], mask_b[:, 0, :, :].rearrange("p j n -> p (j n)"),
                       start=True, stop=False, skip_group_check=True)
                    for j in range(SJ):
                        ins = mm(side[0:PT, j * PT:(j + 1) * PT], q_s[32 * g:32 * g + 32, j * PT:(j + 1) * PT],
                                 k_s[32 * g:32 * g + 32, :], start=False, stop=(j == SJ - 1), skip_group_check=True)
                elif name == "S2":
                    for j in range(SJ):
                        ins = mm(side[:, j * PT:(j + 1) * PT], m_pl[0:PT, j, :], ident[0:PT, 0:PT],
                                 start=True, stop=True)
                elif name == "S3":
                    g = S3_GROUP[step]
                    mm(side[0:PT, 0:SJ * PT], ident_b[0:PT, :], mask_b[:, 1, :, :].rearrange("p j n -> p (j n)"),
                       start=True, stop=False, skip_group_check=True)
                    ins = mm(side[0:PT, 0:SJ * PT], k_s[32 * g:32 * g + 32, :], q_m[32 * g:32 * g + 32, :],
                             start=False, stop=True, skip_group_check=True)
                elif name == "S4":
                    for h in range(SH):
                        g, j = h // SJ, h % SJ
                        ins = mm(side[0:PT, h * (SD + 1):(h + 1) * (SD + 1)], p_s[0:PT, g, j * PT:(j + 1) * PT],
                                 v_s[:, g, :], start=True, stop=True)
                elif name == "S5":
                    ins = nc.tensor.transpose(side[:, 0:PT], o_s[:, :], ident[0:PT, 0:PT])
                elif name == "S6":
                    if isinstance(i, int) and i == -1:
                        pe.wait_ge(swp_ld, 16)
                    ins = mm(side[0:PT, 0:C], o_t[:, :], swp[:, :], start=True, stop=True)
                elif name == "S7":
                    pe.wait_ge(x1_set, i + 2)
                    ins = nc.tensor.transpose(side[:, 0:PT], x1[:, :], ident[0:PT, 0:PT])
                elif name == "S8":
                    s = 0 if step else 1
                    if isinstance(i, int) and i == -1:
                        pe.wait_ge(qk_set, 1)
                    for h in range(XH):
                        ins = mm(side[0:CX, h * T:(h + 1) * T], qk_prod[:, h, :], x1t[:, s * T:(s + 1) * T],
                                 start=True, stop=True)
                elif name == "mrow":
                    pe.wait_ge(negm_set, 2 * i + step // 12 + 2)
                    for r in range(4):
                        ins = mm(side[CX:CX + 1, r * PT:(r + 1) * PT], negm[:, r:r + 1], ident[0:PT, 0:PT],
                                 start=True, stop=True)
                elif name[0] == "Y":
                    if step == 5:
                        pe.wait_ge(u_set, 2 * i)
                    for k, h in enumerate(Y_HEADS[step]):
                        ins = mm(side[0:PT, k * (C + 1):(k + 1) * (C + 1)], u_s[0:CX + 1, h, :], vo_prod[:, h, :],
                                 start=True, stop=True)
                elif name == "X2T":
                    pe.wait_ge(x2_set, i)
                    ins = nc.tensor.transpose(side[:, 0:PT], x2[:, :], ident[0:PT, 0:PT])
                ins.then_inc(side_full, 1)

            def body(i):
                here = parts(i)
                for step in range(24):
                    s, t = step // 12, step % 12
                    if isinstance(i, int) and (i, step) == (-2, 16):
                        pe.wait_ge(xw_ld, 64)
                        weight_product(ps_b[0], wq_f, wk_f, CX)
                    if isinstance(i, int) and (i, step) == (-2, 18):
                        weight_product(ps_b[1][0:CX, :, :], wv_f, wo_f, C)
                    if "main" in here:
                        scores(i, s, t)
                    for at, name, part in SIDE:
                        if at == step and part in here:
                            side_work(i, step, name)
                    if ("second" if s else "main") in here:
                        for k in MAXIMA.get(step, ()):
                            maxima(2 * i + s + 1, 1 - s, k)
                    if step < 4 and "post" in here:
                        sums(2 * i - 1, 1, 4 + t // 2, t % 2)
                    elif step >= 4 and "main" in here:
                        v = step - 4
                        sums(2 * i + v // 12, v // 12, v % 12 // 2, v % 2)

            iterate(pe, body, -2, LOOP_FROM, LOOP_TO, PAIRS + 1)

            pe.wait_ge(side_free, SIDE_END)
            pe.wait_ge(gw_lo_set, 1)
            pe.wait_ge(w_split, PAIRS)
            for c in range(NB):
                wait(pe, lg_set, c - 1)
                if c == 0:
                    pe.wait_ge(a_max, 12 * B)
                dst, cols = ps_a[c % 2][0:EX, 0:FB], slice(c * FB, (c + 1) * FB)
                mm(dst, gw_hl[0][:, :], x2t[0][:, cols], start=True, stop=False)
                mm(dst, gw_hl[0][:, :], x2t[1][:, cols], start=False, stop=False)
                mm(dst, gw_hl[1][:, :], x2t[0][:, cols], start=False, stop=True).then_inc(lg_full, 1)
                pe.wait_ge(lg_set, c + 1)
                for q in range(PPB):
                    ins = nc.tensor.transpose(side_ps[0:PT, (c * PPB + q) * EX:(c * PPB + q + 1) * EX],
                                              lg_t[:, c % 2, q * PT:(q + 1) * PT], ident[0:EX, 0:EX])
            ins.then_inc(side_full, 1)

            w_bank = ps_b[1][:, 0, :]
            fin_bank = ps_b[1][0:PT, 1, :]

            def weights_t():
                pe.wait_ge(gate_step, GATE_STEPS)
                for c in range(NB):
                    wait(pe, wt_set, c)
                    for q in range(PPB):
                        ins = nc.tensor.transpose(w_bank[0:2 * EX, q * PT:(q + 1) * PT], w_hl[:, c * PPB + q, :],
                                                  ident[0:PT, 0:PT])
                    ins.then_inc(wt_full, 1)
                pe.wait_ge(wt_set, NB)

            def expert(c, q):
                e, half = EXPERTS[q // 2], q % 2
                main, late = exists(c, NB), (exists(c, NB) if q >= 3 else exists(c, NB + 1, 1))
                n = UNITS * c + q
                if main:
                    if isinstance(c, int) and c == 0 and q == 2:
                        weights_t()
                    cols = slice((2 * e + half) * 128, (2 * e + half + 1) * 128)
                    moving = [part[:, bass.ds(c * FB, FB)] for part in x2t]
                    if e < EX and half == 0:
                        wait(pe, wb_set, EX * c + e)
                    for dst, w, used, full in ((ps_a[q % 2], wsp[0], silu_set, g_full),
                                               (ps_b[0][:, q % 2, :], wsp[1], hid_set, up_full)):
                        wait(pe, used, n - 1)
                        dst = dst[:, 0:FB]
                        mm(dst, w[0][:, cols], moving[0], start=True, stop=False)
                        mm(dst, w[0][:, cols], moving[1], start=False, stop=False)
                        mm(dst, w[1][:, cols], moving[0], start=False, stop=True).then_inc(full, 1)
                        if w is wsp[0] and e < EX and half == 0:
                            mm(w_bank[:, 0:FB], sel[:, e, :], wt_hl[:, bass.ds(c * FB, FB)],
                               start=True, stop=True).then_inc(wb_full, 1)
                if late:
                    r = (q - 3) % UNITS
                    e, half = EXPERTS[r // 2], r % 2
                    cols = slice((2 * e + half) * 128, (2 * e + half + 1) * 128)
                    pe.wait_ge(hid_lo_set, n - 2)
                    if r == 0:
                        wait(pe, y_set, c)
                    h_hi, h_lo = p_hi[r % 3][:, 0, :], p_lo[r % 3][:, 0, :]
                    dst = ps_u[:, 0:FB]
                    mm(dst, wsp[2][0][:, cols], h_hi, start=(r == 0), stop=False, skip_group_check=True)
                    mm(dst, wsp[2][0][:, cols], h_lo, start=False, stop=False, skip_group_check=True)
                    mm(dst, wsp[2][1][:, cols], h_hi, start=False, stop=(r == UNITS - 1), skip_group_check=True)\
                        .then_inc(down_done, 1)
                if q == 4 and exists(c, NB + 1, 1):
                    pe.wait_ge(y_set, c)
                    wait(pe, fin_set, c - 1)
                    for k in range(PPB):
                        ins = nc.tensor.transpose(fin_bank[:, k * C:(k + 1) * C], y_t[:, k * PT:(k + 1) * PT], ident)
                    ins.then_inc(fin_full, 1)

            def experts(c):
                for q in range(UNITS if exists(c, NB) else 8):
                    expert(c, q)

            iterate(pe, experts, 0, 2, NB, NB + 1)

        @block.scalar
        def _(act):
            act_f = nc.scalar.activation

            def copy(dst, src):
                return act_f(dst, src, ACT.Copy)

            def split_weights(i):
                cols = bass.ds(i * W_PIECE, W_PIECE)
                act.wait_ge(w_ld, 16 * (i + 1))
                copy(w_hi[:, cols], w_raw[:, :]).then_inc(w_hi_set, 1)

            def exp_first(n, u):
                act.wait_ge(b_full, 6 * n + u + 1)
                wait(act, pv_done, 6 * n + u - 2)
                act_f(p_hi[u % 3][0:KT, :, :], ps_b[u % 2][0:KT, :, 0:XR], ACT.Exp, scale=X_SCALE).then_inc(exp_hi, 1)

            def exp_second(n, u):
                act.wait_ge(exp_hi, 6 * n + u + 1)
                b = ps_b[u % 2][0:KT, :, 0:XR]
                act_f(b, b, ACT.Exp, scale=X_SCALE).then_inc(exp_raw, 1)

            def side_work(i, step, name):
                if name in ("S4", "S6", "S1", "S2") or name[0] == "Y":
                    return
                act.wait_ge(side_full, side_count(i, step) + 1)
                side = side_bank(i, step, S3_GROUP[step] if name == "S3" else 0)
                if name == "S0q":
                    copy(q_hi[:, :], side[:, 0:SJ * PT]).then_inc(q_hi_set, 1)
                elif name == "S0k":
                    act_f(k_hi[:, :], side[:, 0:PT], ACT.Identity, bias=k_ones).then_inc(k_hi_set, 1)
                elif name == "S3":
                    act_f(p_s[0:PT, S3_GROUP[step], :], side[0:PT, 0:SJ * PT], ACT.Exp, scale=S_SCALE)\
                        .then_inc(side_free, 1)
                elif name == "S5":
                    copy(o_t[:, :], side[:, 0:PT]).then_inc(side_free, 1)
                elif name == "S7":
                    copy(x1t[:, :], side[:, 0:PT]).then_inc(side_free, 1)
                elif name == "S8":
                    copy(xq_hi[0:CX, 1 - step // 12, :], side[0:CX, 0:XR]).then_inc(xq_hi_set, 1)
                elif name == "mrow":
                    copy(xq_hi[CX:CX + 1, 1 - step // 12, :], side[CX:CX + 1, 0:XR]).then_inc(side_free, 1)
                elif name == "X2T":
                    copy(x2t[0][:, bass.ds((i - 1) * PT, PT)], side[:, 0:PT]).then_inc(x2t_hi_set, 1)

            def split_ct(n, s, c):
                act.wait_ge(ct_ld[c], 16 * (n + 1))
                wait(act, b_full, 6 * (n - 2) + 2 * c + 2)
                copy(ct_hi[0:CX, s, c * CHUNK:(c + 1) * CHUNK], ct_raw[0:CX, c, :]).then_inc(cthi_set, 1)

            def split_v(n, s, part):
                tiles = slice(part * 4, part * 4 + 4)
                if part == 0:
                    act.wait_ge(v_ld, 16 * (n + 1))
                    wait(act, pv_done, 6 * (n - 1))
                copy(v_hi[:, s, tiles, 0:CX], v_raw_t[:, tiles, :]).then_inc(vhi_set, 1)

            def save_sums(n, s):
                act.wait_ge(pv_done, 6 * (n + 1))
                copy(u_s[0:CX + 1, :, s * T:(s + 1) * T],
                     ps_u[0:CX + 1, 0:XR].rearrange("p (h t) -> p h t", h=XH)).then_inc(u_set, 1)

            def body(i):
                here = parts(i)
                for step in range(24):
                    s, t = step // 12, step % 12
                    if isinstance(i, int) and (i, step) == (-2, 17):
                        act.wait_ge(prod_full, 1)
                        copy(qk_prod[:, :, :].rearrange("p (a h) c -> p a (h c)", a=2), ps_b[0][:, :, 0:4 * CX])\
                            .then_inc(qk_set, 1)
                    if isinstance(i, int) and (i, step) == (-1, 13):
                        act.wait_ge(gw_ld, 16)
                        copy(gw_hl[0][:, :], gw[:, :]).then_inc(gw_hi_set, 1)
                    if t % 2 and "main" in here:
                        exp_first(2 * i + s, t // 2)
                    if t % 2 == 0:
                        if step == 0 and "post" in here:
                            exp_second(2 * i - 1, 5)
                        elif step and "main" in here:
                            exp_second(2 * i + (step - 1) // 12, (t // 2 - 1) % 6)
                    if step == 4 and "post" in here:
                        save_sums(2 * i - 1, 1)
                    if step == 16 and "main" in here:
                        save_sums(2 * i, 0)
                    for at, name, part in SIDE:
                        if at == step and part in here:
                            side_work(i, step, name)
                    if step == W_STEP and "main" in here:
                        split_weights(i)
                    n = 2 * i + s
                    if isinstance(i, int) and i == -2:
                        continue
                    if t == 0 and exists(n + 1):
                        split_ct(n + 1, 1 - s, 2)
                    if t in (4, 8) and exists(n + 2):
                        split_ct(n + 2, s, t // 4 - 1)
                    if t in (5, 7, 10) and exists(n + 1):
                        split_v(n + 1, 1 - s, (5, 7, 10).index(t))

            iterate(act, body, -2, LOOP_FROM, LOOP_TO, PAIRS + 1)

            for c in range(NB):
                act.wait_ge(lg_full, c + 1)
                copy(lg_t[:, c % 2, :], ps_a[c % 2][0:EX, 0:FB]).then_inc(lg_set, 1)
            act.wait_ge(gate_step, 2)
            act_f(gt[:, 1, :, :], gt[:, 0, :, :], ACT.Exp).then_inc(gate_exp, 1)

            def expert(c, q):
                e, half = EXPERTS[q // 2], q % 2
                n = UNITS * c + q
                if exists(c, NB):
                    if isinstance(c, int) and c == 0 and q == 2:
                        for k in range(NB):
                            act.wait_ge(wt_full, k + 1)
                            copy(wt_hl[:, k * FB:(k + 1) * FB], ps_b[1][0:2 * EX, 0, 0:FB]).then_inc(wt_set, 1)
                    act.wait_ge(g_full, n + 1)
                    wait(act, hid_set, n - 1)
                    act_f(silu_s[:, q % 2, :], ps_a[q % 2][:, 0:FB], ACT.Silu).then_inc(silu_set, 1)
                    if e < EX and half == 0:
                        act.wait_ge(wb_full, EX * c + e + 1)
                        wait(act, weighted, 2 * (EX * c + e - 1))
                        copy(wgt_b[:, e % 2, :], ps_b[1][:, 0, 0:FB]).then_inc(wb_set, 1)
                if exists(c, NB) if q else exists(c, NB + 1, 1):
                    r = (q - 1) % UNITS
                    act.wait_ge(hid_set, n)
                    wait(act, down_done, n - 3)
                    copy(p_hi[r % 3][:, 0, :], hid[:, r % 2, :]).then_inc(hid_hi_set, 1)
                if q == 3 and exists(c, NB + 1, 1):
                    act.wait_ge(down_done, UNITS * c)
                    wait(act, fin_full, c - 1)
                    copy(y_t, ps_u[:, 0:FB]).then_inc(y_set, 1)

            def experts(c):
                for q in range(UNITS if exists(c, NB) else 8):
                    expert(c, q)

            iterate(act, experts, 0, 2, NB, NB + 1)

        @block.vector
        def _(dve):
            tt, ts, stt, cp = nc.vector.tensor_tensor, nc.vector.tensor_scalar, nc.vector.scalar_tensor_tensor, \
                nc.vector.tensor_copy
            dve.wait_ge(sw_ld, 32)
            dve.wait_ge(zeroed, 8)
            for r in range(3):
                cp(wq_pad[:, :, :, r * SD:(r + 1) * SD],
                   swq[:, :, :, :].rearrange("c g j d -> c j g d")).then_inc(pads_set, 1)
                cp(wk_pad[:, :, r * SD:(r + 1) * SD], swkv[:, 0, :, :]).then_inc(pads_set, 1)
            dve.wait_ge(cst_ld, 16)
            cp(ident_b[:, :], ident[:, 0:PT]).then_inc(masks_set, 1)
            for m in range(2):
                cp(mask_b[:, m, :, :], over(cst[0:PT, None, 131 + m * PT:131 + (m + 1) * PT], [PT, SJ, PT]))\
                    .then_inc(masks_set, 1)

            def lo_parts(i, step):
                if step == 0 and "post" in parts(i):
                    probs_lo(2 * i - 1, 5)
                elif step and "main" in parts(i):
                    probs_lo(2 * i + (step - 1) // 12, (step % 12 // 2 - 1) % 6)

            def maxima(n, k):
                dve.wait_ge(a_full, 12 * n + k + 1)
                nc.vector.tensor_reduce(mx[:, k % 4, k // 4:k // 4 + 1], ps_a[k % 2][0:PT, 0:CHUNK], AX.X,
                                        ALU.max).then_inc(a_max, 1)
                if k == 11:
                    dve.wait_ge(a_max, 12 * (n + 1))
                    nc.vector.tensor_reduce(negm[:, :], mx[:, :, :], AX.X, ALU.max, negate=True).then_inc(negm_set, 1)

            def probs_lo(n, u):
                dve.wait_ge(exp_raw, 6 * n + u + 1)
                tt(p_lo[u % 3][0:KT, :, :], ps_b[u % 2][0:KT, :, 0:XR], bits(p_hi[u % 3][0:KT, :, :]),
                   ALU.subtract).then_inc(plo_set, 1)

            def statistics(src, st, mv, n, st_set, mv_set):
                nc.vector.bn_stats(st[:, :], src[:, :]).then_inc(st_set, 1)
                dve.wait_ge(st_set, n)
                take_wait(nc.vector)
                nc.vector.bn_aggr(mv[:, :], st[:, :]).then_inc(mv_set, 1)

            def side_work(i, step, name):
                use = side_count(i, step)
                side = side_bank(i, step, S1_GROUP[step] if name == "S1" else 0)
                if name in ("S3", "S5", "S7", "mrow"):
                    return
                if name not in ("S0q", "S0k", "S8", "X2T"):
                    dve.wait_ge(side_full, use + 1)
                if name == "S0q":
                    dve.wait_ge(q_hi_set, i + 3)
                    stt(q_s[:, :], bits(q_hi[:, :]), q_part, side[:, 0:SJ * PT], ALU.mult, ALU.add)\
                        .then_inc(side_free, 1)
                elif name == "S0k":
                    dve.wait_ge(k_hi_set, i + 3)
                    stt(k_s[:, :], bits(k_hi[:, :]), k_part, side[:, 0:PT], ALU.mult, ALU.add)
                    cp(v_s[:, :, 0:SD], side[0:PT, 128:128 + SG * SD].rearrange("p (g d) -> p g d", g=SG))\
                        .then_inc(side_free, 1)
                elif name == "S1":
                    at = 32 * S1_GROUP[step] + MAX_ROW
                    nc.vector.tensor_reduce(m_pl[0:PT, :, at:at + 1],
                                            side[0:PT, 0:SJ * PT].rearrange("p (j n) -> p j n", j=SJ), AX.X, ALU.max,
                                            negate=True).then_inc(side_free, 1)
                elif name == "S2":
                    tt(q_m[:, :], side[:, 0:SJ * PT], bits(q_s[:, :]), ALU.add).then_inc(side_free, 1)
                elif name == "S4":
                    o = side[0:PT, 0:SH * (SD + 1)].rearrange("p (h d) -> p h d", h=SH)
                    nc.vector.reciprocal(rl_s[:, :], side[0:PT, SD:SH * (SD + 1):SD + 1]).then_inc(rl_set, 1)
                    dve.wait_ge(rl_set, i + 2)
                    tt(o_s[:, :].rearrange("p (h d) -> p h d", h=SH), o[:, :, 0:SD],
                       over(rl_s[:, :, None], [PT, SH, SD]), ALU.mult).then_inc(side_free, 1)
                elif name == "S6":
                    dve.wait_ge(xr_set, i + 2)
                    tt(r1[:, :], side[0:PT, 0:C], xr[:, :], ALU.add).then_inc(side_free, 1)
                elif name == "S8":
                    buffer = 1 - step // 12
                    dve.wait_ge(xq_hi_set, 2 * i + step // 12 + 2)
                    tt(xq_lo[:, buffer, :], side[0:CX, 0:XR], bits(xq_hi[0:CX, buffer, :]), ALU.subtract)\
                        .then_inc(side_free, 1)
                elif name[0] == "Y":
                    heads = Y_HEADS[step]
                    first, count = heads[0], len(heads)
                    if step == 5:
                        wait(dve, y_summed, 4 * (i - 1))
                    nc.vector.reciprocal(ry[:, 0:count], side[0:PT, C:count * (C + 1):C + 1]).then_inc(ry_set, 1)
                    dve.wait_ge(ry_set, 3 * (i - 1) + list(Y_HEADS).index(step) + 1)
                    tt(y_h[:, first:first + count, :],
                       side[0:PT, 0:count * (C + 1)].rearrange("p (h c) -> p h c", h=count)[:, :, 0:C],
                       over(ry[:, 0:count, None], [PT, count, C]), ALU.mult).then_inc(side_free, 1)
                elif name == "X2T":
                    dve.wait_ge(x2t_hi_set, i)
                    cols = bass.ds((i - 1) * PT, PT)
                    tt(x2t[1][:, cols], side[:, 0:PT], bits(x2t[0][:, cols]), ALU.subtract).then_inc(side_free, 1)

            def body(i):
                here = parts(i)
                for step in range(24):
                    s, t = step // 12, step % 12
                    if isinstance(i, int) and (i, step) == (-2, 19):
                        dve.wait_ge(prod_full, 2)
                        cp(vo_prod[0:CX, :, 0:C], ps_b[1][0:CX, :, :].rearrange("p a (h c) -> p (a h) c", h=4))\
                            .then_inc(vo_set, 1)
                        nc.vector.memset(vo_prod[CX:CX + 1, :, 0:C], 0.0).then_inc(rows_set, 1)
                        nc.vector.memset(vo_prod[CX:CX + 1, :, C:C + 1], 1.0).then_inc(rows_set, 1)
                    if isinstance(i, int) and i == -1 and step in (3, 5):
                        buffer = (step - 3) // 2
                        nc.vector.memset(bits(ct_hi[CX:CX + 1, buffer, :]), 1.0).then_inc(rows_set, 1)
                    if isinstance(i, int) and (i, step) == (-1, 14):
                        dve.wait_ge(gw_hi_set, 1)
                        tt(gw_hl[1][:, :], gw[:, :], bits(gw_hl[0][:, :]), ALU.subtract).then_inc(gw_lo_set, 1)
                    if t % 2 == 0 and step not in SIDE_FIRST:
                        lo_parts(i, step)
                    for at, name, part in SIDE:
                        if at == step and part in here:
                            side_work(i, step, name)
                    if step == 9 and "second" in here:
                        dve.wait_ge(side_free, side_count(i, 8) + 1)
                        statistics(r1, st1, mv1, i + 2, st1_set, mv1_set)
                    if step == 10 and "second" in here:
                        dve.wait_ge(rstd1_set, i + 2)
                        wait(dve, xb_set, i + 1)
                        ts(x1[:, :], r1[:, :], mv1[:, 0:1], rstd1[:, 1:2], ALU.subtract, ALU.mult).then_inc(x1_set, 1)
                    if step in SIDE_FIRST:
                        lo_parts(i, step)
                    if step == 15 and "post" in here:
                        dve.wait_ge(y_summed, 4 * i)
                        statistics(acc, st2, mv2, i, st2_set, mv2_set)
                    if step == 16 and "post" in here:
                        dve.wait_ge(rstd2_set, i)
                        wait(dve, x2_kept, i - 1)
                        ts(x2[:, :], acc[:, :], mv2[:, 0:1], rstd2[:, 1:2], ALU.subtract, ALU.mult).then_inc(x2_set, 1)
                    if ("second" if s else "main") in here:
                        for k in MAXIMA.get(step, ()):
                            maxima(2 * i + s + 1, k)

            iterate(dve, body, -2, LOOP_FROM, LOOP_TO, PAIRS + 1)

            steps = [0]

            def step(ins):
                steps[0] += 1
                ins.then_inc(gate_step, 1)
                dve.wait_ge(gate_step, steps[0])

            tt(sel, over(ident[0:2 * EX, 0:EX, None], [2 * EX, EX, 128]),
               over(ident[0:2 * EX, EX:2 * EX, None], [2 * EX, EX, 128]), ALU.add).then_inc(sel_set, 1)
            dve.wait_ge(side_full, SIDE_END + 1)
            logits = side_ps[0:PT, 0:PAIRS * EX].rearrange("p (q e) -> p q e", q=PAIRS)
            full = [PT, PAIRS, EX]
            step(nc.vector.tensor_reduce(g1[:, 0, :], logits, AX.X, ALU.max, negate=True))
            step(tt(gt[:, 0, :, :], logits, over(g1[:, 0, :, None], full), ALU.add))
            dve.wait_ge(gate_exp, 1)
            step(nc.vector.tensor_reduce(g1[:, 1, :], gt[:, 1, :, :], AX.X, ALU.add))
            step(nc.vector.reciprocal(g1[:, 2, :], g1[:, 1, :]))
            step(tt(gt[:, 2, :, :], gt[:, 1, :, :], over(g1[:, 2, :, None], full), ALU.mult))
            for q in range(PAIRS):
                ins = nc.vector.max(gt[:, 3, q, :], gt[:, 2, q, :])
            step(ins)
            for q in range(PAIRS):
                ins = nc.vector.max_index(gi[:, q, :], gt[:, 3, q, :], gt[:, 2, q, :])
            step(ins)
            step(cp(gt[:, 4, :, :], gi[:, :, :]))
            step(tt(g1[:, 3, :], gt[:, 3, :, 0], gt[:, 3, :, 1], ALU.add))
            step(ts(g1[:, 4, :], g1[:, 3, :], 1e-20, None, ALU.add))
            step(nc.vector.reciprocal(g1[:, 5, :], g1[:, 4, :]))
            for k in range(2):
                step(tt(g1[:, 6, :], gt[:, 3, :, k], g1[:, 5, :], ALU.mult))
                step(tt(gt[:, 5 + k, :, :], over(iota8[:, None, :], full), over(gt[:, 4, :, k:k + 1], full),
                        ALU.is_equal))
                step(tt(gt[:, 5 + k, :, :], gt[:, 5 + k, :, :], over(g1[:, 6, :, None], full), ALU.mult))
            step(tt(gt[:, 7, :, :], gt[:, 5, :, :], gt[:, 6, :, :], ALU.add))
            step(cp(w_h[:, :, :], gt[:, 7, :, :]))
            step(cp(w_hl[:, :, 0:EX], bits(w_h[:, :, :])))
            step(tt(w_hl[:, :, EX:2 * EX], gt[:, 7, :, :], bits(w_h[:, :, :]), ALU.subtract))
            assert steps[0] == GATE_STEPS

            def expert(c, q):
                e = EXPERTS[q // 2]
                n = UNITS * c + q
                if exists(c, NB):
                    if e < EX:
                        dve.wait_ge(weighted, 2 * EX * c + q - 1)
                    else:
                        dve.wait_ge(silu_set, n + 1)
                    dve.wait_ge(up_full, n + 1)
                    wait(dve, hid_lo_set, n - 1)
                    tt(hid[:, q % 2, :], silu_s[:, q % 2, :], ps_b[0][:, q % 2, 0:FB], ALU.mult).then_inc(hid_set, 1)
                if exists(c, NB) if q else exists(c, NB + 1, 1):
                    r = (q - 1) % UNITS
                    dve.wait_ge(hid_hi_set, n)
                    tt(p_lo[r % 3][:, 0, :], hid[:, r % 2, :], bits(p_hi[r % 3][:, 0, :]), ALU.subtract)\
                        .then_inc(hid_lo_set, 1)
                if q == 5 and exists(c, NB + 1, 1):
                    dve.wait_ge(fin_full, c)
                    tt(fin[:, :, :].rearrange("p q n -> p (q n)"), ps_b[1][0:PT, 1, :],
                       x_rows[:, bass.ds((c - 1) * PPB * C, PPB * C)], ALU.add).then_inc(fin_set, 1)
                    dve.wait_ge(fin_set, c)
                    for k in range(PPB):
                        ins = nc.vector.bn_stats(st3[:, k, :], fin[:, k, :])
                    ins.then_inc(st3_set, 1)
                    dve.wait_ge(st3_set, c)
                    take_wait(nc.vector)
                    for k in range(PPB):
                        ins = nc.vector.bn_aggr(mv3[:, k, :], st3[:, k, :])
                    ins.then_inc(mv3_set, 1)
                if q == 7 and exists(c, NB + 1, 1):
                    dve.wait_ge(rstd3_set, c)
                    wait(dve, out_st, 16 * (c - 1))
                    for k in range(PPB):
                        ts(out_s[:, k, :], fin[:, k, :], mv3[:, k, 0:1], rstd3[:, 1, k:k + 1],
                           ALU.subtract, ALU.mult).then_inc(out_set, 1)

            def experts(c):
                for q in range(UNITS if exists(c, NB) else 8):
                    expert(c, q)

            iterate(dve, experts, 0, 2, NB, NB + 1)

        @block.gpsimd
        def _(pool):
            ptt, pcp, fill = nc.gpsimd.tensor_tensor, nc.gpsimd.tensor_copy, nc.gpsimd.memset
            for ap, value in ((wq_pad[:, :, :, :], 0.0), (wk_pad[:, :, :], 0.0), (m_pl[:, :, :], 0.0),
                              (v_s[:, :, :], 1.0), (eps[:, :], EPS), (nhalf[:, :], -0.5),
                              (vo_prod[0:CX, :, C:C + 1], 0.0), (bits(v_hi[:, :, :, CX:CX + 1]), 1.0)):
                fill(ap, value).then_inc(zeroed, 1)
            pool.wait_ge(zeroed, 8)

            def split_ct(n, s, c):
                cols = slice(c * CHUNK, (c + 1) * CHUNK)
                pool.wait_ge(cthi_set, 3 * n + c + 1)
                ptt(ct_lo[:, s, cols], ct_raw[0:CX, c, :], bits(ct_hi[0:CX, s, cols]), ALU.subtract)\
                    .then_inc(ctlo_set, 1)

            def split_v(n, s, part):
                tiles = slice(part * 4, part * 4 + 4)
                pool.wait_ge(vhi_set, 3 * n + part + 1)
                ins = ptt(v_lo[:, s, tiles, :], v_raw_t[:, tiles, :], bits(v_hi[:, s, tiles, 0:CX]), ALU.subtract)
                if part == 2:
                    ins.then_inc(vlo_set, 1)

            def rstd(out2, var, n, ve_set, done):
                width = out2[0].shape[-1]
                ptt(out2[0], var, eps[0:PT, 0:width], ALU.add).then_inc(ve_set, 1)
                pool.wait_ge(ve_set, n)
                ptt(out2[1], out2[0], nhalf[0:PT, 0:width], ALU.pow).then_inc(done, 1)

            def body(i):
                here = parts(i)
                for step in range(0 if isinstance(i, int) and i == -2 else 24):
                    s, t = step // 12, step % 12
                    n = 2 * i + s
                    if t == 0 and exists(n + 1):
                        split_ct(n + 1, 1 - s, 2)
                    if t in (4, 8) and exists(n + 2):
                        split_ct(n + 2, s, t // 4 - 1)
                    if t in (5, 7, 10) and exists(n + 1):
                        split_v(n + 1, 1 - s, (5, 7, 10).index(t))
                    if step == W_STEP + 1 and "main" in here:
                        cols = bass.ds(i * W_PIECE, W_PIECE)
                        pool.wait_ge(w_hi_set, i + 1)
                        ptt(w_lo[:, cols], w_raw[:, :], bits(w_hi[:, cols]), ALU.subtract).then_inc(w_split, 1)
                    if step == 3 and "second" in here:
                        if isinstance(i, int) and i == -1:
                            pool.wait_ge(bias_ld, 16)
                        pool.wait_ge(xn_ld, 16 * (i + 2))
                        wait(pool, mv1_set, i + 1)
                        ptt(xr[:, :], xn[:, :], bias2[:, 0, :], ALU.add).then_inc(xr_set, 1)
                    if step == 9 and "second" in here:
                        pool.wait_ge(mv1_set, i + 2)
                        rstd((rstd1[:, 0:1], rstd1[:, 1:2]), mv1[:, 1:2], i + 2, ve1_set, rstd1_set)
                    if step == 11 and "second" in here:
                        pool.wait_ge(x1_set, i + 2)
                        ptt(x_rows[:, bass.ds((i + 1) * C, C)], x1[:, :], bias2[:, 1, :], ALU.add).then_inc(xb_set, 1)
                    if step == 12 and "post" in here:
                        pool.wait_ge(side_free, side_count(i, 9) + 1)
                        for k, half in enumerate((4, 2, 1)):
                            ptt(y_h[:, 0:half, :], y_h[:, 0:half, :], y_h[:, half:2 * half, :], ALU.add)\
                                .then_inc(y_summed, 1)
                            pool.wait_ge(y_summed, 4 * (i - 1) + k + 1)
                        wait(pool, x2_set, i - 1)
                        ptt(acc[:, :], y_h[:, 0, :], x_rows[:, bass.ds((i - 1) * C, C)], ALU.add)\
                            .then_inc(y_summed, 1)
                    if step == 15 and "post" in here:
                        pool.wait_ge(mv2_set, i)
                        rstd((rstd2[:, 0:1], rstd2[:, 1:2]), mv2[:, 1:2], i, ve2_set, rstd2_set)
                    if step == 16 and "post" in here:
                        pool.wait_ge(x2_set, i)
                        take_wait(nc.gpsimd)
                        pcp(x_rows[:, bass.ds((i - 1) * C, C)], x2[:, :]).then_inc(x2_kept, 1)

            iterate(pool, body, -2, LOOP_FROM, LOOP_TO, PAIRS + 1)

            def expert(c, q):
                e, half = EXPERTS[q // 2], q % 2
                if exists(c, NB) and e < EX:
                    pool.wait_ge(silu_set, UNITS * c + q + 1)
                    pool.wait_ge(wb_set, EX * c + e + 1)
                    ptt(silu_s[:, q % 2, :], silu_s[:, q % 2, :], wgt_b[:, e % 2, :], ALU.mult).then_inc(weighted, 1)
                if q == 6 and exists(c, NB + 1, 1):
                    pool.wait_ge(mv3_set, c)
                    rstd((rstd3[:, 0, :], rstd3[:, 1, :]), mv3[:, :, 1], c, ve3_set, rstd3_set)

            def experts(c):
                for q in range(UNITS if exists(c, NB) else 8):
                    expert(c, q)

            iterate(pool, experts, 0, 2, NB, NB + 1)


def constants():
    cst = np.zeros((128, CONST_COLS), np.float32)
    cst[:, 0:128] = np.eye(128)
    row = np.arange(128) % 32
    cst[:, 128] = np.where((row >= SD) & (row < 2 * SD), -1.0, 0.0)
    cst[:, 129] = np.where((row >= 2 * SD) & (row < 3 * SD), -1.0, 0.0)
    cst[:, 129] += np.where(row == MAX_ROW, 1.0, 0.0)
    cst[:, 130] = np.where(row == MAX_ROW, 1.0, 0.0)
    q, k = np.arange(PT)[:, None], np.arange(PT)[None, :]
    mask = np.where((q // T == k // T) & (k <= q), 0.0, MASKED)
    cst[0:PT, 131:131 + PT] = mask
    cst[0:PT, 131 + PT:131 + 2 * PT] = mask.T
    cst[:, 131 + 2 * PT:] = np.arange(EX)
    return cst


def kernel(**inputs):
    import concourse.bacc as bacc
    from concourse.bass_utils import run_bass_kernel_spmd

    a = {n: np.asarray(v) for n, v in inputs.items()}
    x = a["x"].reshape(B * T, C)
    context = a["ctx_768"].reshape(B, KT, NT, CX)
    shared = {n: a["L0_ffn_ws_" + n] for n in ("gate", "up", "down")}
    wide = {n: np.concatenate([a["L0_ffn_w_" + n], shared[n][None]]).transpose(1, 0, 2).reshape(C, -1)
            for n in ("gate", "up")}
    down = np.concatenate([a["L0_ffn_w_down"], shared["down"][None]]).reshape(EX + 1, 2, 128, C)
    s_bias = np.concatenate([a["L0_attn_bp"], a["L0_xattn_bo"]])
    arrays = {
        "x_t": x.T, "x_n": x,
        "ctx_n": context.reshape(B * KT, NT * CX),
        "ctx_t": context.transpose(0, 3, 2, 1).reshape(B * CX, KV),
        "s_wq_t": a["L0_attn_Wq"].reshape(SH * SD, C).T,
        "s_wkv_t": np.concatenate([a["L0_attn_Wk"].reshape(SG * SD, C), a["L0_attn_Wv"].reshape(SG * SD, C)]).T,
        "s_wp_t": a["L0_attn_Wp"].T,
        "s_bias": np.broadcast_to(s_bias, (PT, 2 * C)),
        "x_wq_t": a["L0_xattn_Wq"].T, "x_wk_t": a["L0_xattn_Wk"].T, "x_wv_t": a["L0_xattn_Wv"].T,
        "x_wo": a["L0_xattn_Wo"],
        "gate_w": a["L0_ffn_gate_w"],
        "w_all": np.concatenate([wide["gate"], wide["up"], down.transpose(2, 0, 1, 3).reshape(128, -1)], axis=1),
        "consts": constants(),
    }
    nc = bacc.Bacc("TRN2", target_bir_lowering=False, num_devices=1)
    feeds, args = {}, []
    for name, value in arrays.items():
        value = np.ascontiguousarray(value)
        feeds["in_" + name] = value
        args.append(nc.dram_tensor("in_" + name, value.shape, mybir.dt.from_np(value.dtype), kind="ExternalInput").ap())
    out = nc.dram_tensor("out", (B * T, C), F32, kind="ExternalOutput").ap()
    bass_decoder_layer(nc, *args, out)
    result = run_bass_kernel_spmd(nc, [feeds], core_ids=[0])
    return result.results[0]["out"].reshape(B, T, C)
```

```python
from contextlib import ExitStack

import numpy as np
import concourse.bass as bass
from concourse import mybir

ALU = mybir.AluOpType
ACT = mybir.ActivationFunctionType
F32 = mybir.dt.float32
F32R = mybir.dt.float32r
BF16 = mybir.dt.bfloat16
U32 = mybir.dt.uint32
AX = mybir.AxisListType

B, T, C = 32, 56, 128
PT = 2 * T
PAIRS = B // 2
KV, CX = 1500, 96
KT, NT = 125, 12
CHUNK = 4 * KT
XH, XD = 8, 64
XR = XH * T
SH, SG, SJ, SD = 16, 4, 4, 8
EX, ED = 8, 256
FB = 448
NB = B * T // FB
PPB = FB // PT
EPS = 1e-5
S_SCALE = SD ** -0.5
X_SCALE = XD ** -0.5
MASKED = -1e30
MAX_ROW = 24

SIDE = [(0, "S8", "main"), (1, "S3", "second"), (2, "S3", "second"), (4, "S4", "second"),
        (5, "Y0", "post"), (6, "S5", "second"), (7, "Y1", "post"), (8, "S6", "second"),
        (9, "Y2", "post"), (10, "mrow", "main"), (11, "S7", "second"), (12, "S8", "second"),
        (13, "S0q", "first"), (14, "S0k", "first"), (15, "S1", "first"), (16, "S1", "first"),
        (17, "S1", "first"), (18, "S1", "first"), (19, "X2T", "post"), (20, "S2", "first"),
        (21, "S3", "first"), (22, "mrow", "second"), (23, "S3", "first")]
S0K_STEP = 14
S1_GROUP = {15: 0, 16: 1, 17: 2, 18: 3}
S3_GROUP = {21: 0, 23: 1, 1: 2, 2: 3}
Y_HEADS = {5: (0, 1, 2), 7: (3, 4, 5), 9: (6, 7)}
MAXIMA = {1: (0, 1), 2: (2, 3), 3: (4, 5), 4: (6,), 5: (7, 8), 6: (9,), 7: (10, 11),
          13: (0, 1), 14: (2,), 15: (3,), 16: (4,), 17: (5, 6), 18: (7,), 19: (8, 9), 20: (10, 11)}
SIDE_FIRST = (0, 8, 10, 12, 14, 16, 20)
LOOP_FROM, LOOP_TO = 2, PAIRS - 2


def parts(i):
    if not isinstance(i, int):
        return {"main", "post", "second", "first"}
    return {name for name, lo, hi in (("main", 0, PAIRS), ("post", 1, PAIRS + 1),
                                      ("second", -1, PAIRS - 1), ("first", -2, PAIRS - 2))
            if lo <= i < hi}


def side_count(i, step):
    here = sum(1 for s, _, part in SIDE if s < step and part in parts(i))
    if not isinstance(i, int):
        return len(SIDE) * i + (side_count(LOOP_FROM, 0) - len(SIDE) * LOOP_FROM + here)
    return here + sum(1 for j in range(-2, i) for _, _, part in SIDE if part in parts(j))


def side_count_before(i, step):
    if isinstance(i, int):
        return side_count(i - 1, step)
    return side_count(i, 0) - sum(1 for s, _, _ in SIDE if s >= step)


SIDE_END = side_count(PAIRS + 1, 0)
EW = (EX + 1) * ED
W_PIECE = 3 * EW // PAIRS
W_STEP = 11
EXPERTS = (EX,) + tuple(range(EX))
UNITS = 2 * len(EXPERTS)
GATE_PAIRS = ((0, PAIRS - PPB), (PAIRS - PPB, PAIRS))
GATE_STAGES = {12: "logits", 13: "differences", 14: "exponentials", 15: "probabilities", 16: "largest",
               17: "shares", 18: "first", 19: "second", 20: "split"}
GATE_UNITS = {11: "logits", 12: "differences", 13: "exponentials", 14: "probabilities", 15: "largest",
              16: "shares", 17: "first", 19: "second", 20: "split"}
GATE_LINKS = {"differences": 2, "probabilities": 3, "largest": 2, "shares": 4, "first": 3, "second": 3, "split": 4}
ALL_LINKS = sum(GATE_LINKS.values())
LAST_STEPS = {0: 5, 1: 7, 2: 9, 3: 12, 4: 13, 5: 15, 6: 16, 7: 17, 8: 18, 9: 19}
CONST_COLS = 128 + 3 + 2 * PT + EX


def bass_decoder_layer(nc, x_t, x_n, ctx_n, ctx_t, s_wq_t, s_wkv_t, s_wp_t, s_bias, x_wq_t, x_wk_t, x_wv_t,
                       x_wo, gate_w, w_all, consts, out):
    with ExitStack() as ctx:
        def sb(name, shape, dt=F32):
            return ctx.enter_context(nc.sbuf_tensor(name, shape, dt))

        def ps(name, shape):
            return ctx.enter_context(nc.psum_tensor(name, shape, F32))

        def sem(name):
            return ctx.enter_context(nc.semaphore(name))

        cst = sb("cst", [128, CONST_COLS])
        ident = cst[:, 0:128]
        q_part, k_part, k_ones = (cst[:, 128 + n:129 + n] for n in range(3))
        iota8 = cst[0:PT, 131 + 2 * PT:139 + 2 * PT]
        ident_b = sb("ident_b", [128, PT], BF16)
        mask_b = sb("mask_b", [PT, 2, SJ, PT], BF16)
        eps = sb("eps", [128, 4])
        nhalf = sb("nhalf", [128, 4])
        spare = sb("spare", [128, 32])
        taken = [0]
        swq = sb("swq", [128, SG, SJ, SD])
        swkv = sb("swkv", [128, 2, SG, SD])
        swp = sb("swp", [128, C])
        bias2 = sb("bias2", [PT, 2, C])
        wq_pad = sb("wq_pad", [128, SJ, SG, 32])
        wk_pad = sb("wk_pad", [128, SG, 32])
        qk_prod = sb("qk_prod", [128, XH, CX])
        vo_prod = sb("vo_prod", [CX + 1, XH, C + 1])
        gw = sb("gw", [128, EX])
        gw_hl = [sb(f"gw_{p}", [128, EX], F32R) for p in ("hi", "lo")]
        w_hi = sb("w_hi", [128, 3 * EW], F32R)
        w_lo = sb("w_lo", [128, 3 * EW], F32R)
        w_raw = sb("w_raw", [128, W_PIECE])
        wsp = [[part[:, n * EW:(n + 1) * EW] for part in (w_hi, w_lo)] for n in range(3)]
        x_rows = sb("x_rows", [PT, PAIRS * C])
        x2t = [sb(f"x2t_{p}", [128, B * T], F32R) for p in ("hi", "lo")]
        xt = sb("xt", [128, PT])
        xn = sb("xn", [PT, C])
        xr = sb("xr", [PT, C])
        q_hi = sb("q_hi", [128, SJ * PT], F32R)
        q_s = sb("q_s", [128, SJ * PT], F32R)
        q_m = sb("q_m", [128, SJ * PT], F32R)
        k_hi = sb("k_hi", [128, PT], F32R)
        k_s = sb("k_s", [128, PT], F32R)
        v_s = sb("v_s", [PT, SG, SD + 1])
        m_pl = sb("m_pl", [128, SJ, 128])
        p_s = sb("p_s", [128, SG, SJ * PT])
        rl_s = sb("rl_s", [PT, SH])
        o_s = sb("o_s", [PT, C])
        o_t = sb("o_t", [C, PT])
        r1 = sb("r1", [PT, C])
        st1 = sb("st1", [PT, 6])
        mv1 = sb("mv1", [PT, 2])
        rstd1 = sb("rstd1", [PT, 2])
        x1 = sb("x1", [PT, C])
        x1t = sb("x1t", [C, PT])
        ct_raw = sb("ct_raw", [128, 3, CHUNK])
        ct_hi = sb("ct_hi", [CX + 1, 2, 3 * CHUNK], F32R)
        ct_lo = sb("ct_lo", [CX, 2, 3 * CHUNK], F32R)
        v_raw = sb("v_raw", [128, NT * CX])
        v_raw_t = v_raw[0:KT, :].rearrange("p (t c) -> p t c", t=NT)
        v_hi = sb("v_hi", [KT, 2, NT, CX + 1], F32R)
        v_lo = sb("v_lo", [KT, 2, NT, CX], F32R)
        xq_hi = sb("xq_hi", [CX + 1, 2, XR], F32R)
        xq_lo = sb("xq_lo", [CX, 2, XR], F32R)
        mx = sb("mx", [PT, 4, 3])
        negm = sb("negm", [PT, 4])
        p_hi = [sb(f"p_hi{n}", [128, 2, XR], F32R) for n in range(3)]
        p_lo = [sb(f"p_lo{n}", [128, 2, XR], F32R) for n in range(3)]
        u_s = sb("u_s", [128, XH, PT])
        ry = sb("ry", [PT, 4])
        y_h = sb("y_h", [PT, XH, C])
        acc = sb("acc", [PT, C])
        st2 = sb("st2", [PT, 6])
        mv2 = sb("mv2", [PT, 2])
        rstd2 = sb("rstd2", [PT, 2])
        x2 = sb("x2", [PT, C])
        ct_flat = ct_raw[:, :, :].rearrange("p c n -> p (c n)")
        u_flat = u_s[:, :, :].rearrange("p h n -> p (h n)")
        p_flat = p_s[0:PT, :, :].rearrange("p g n -> p (g n)")
        silu_s = ct_flat[:, 0:2 * FB].rearrange("p (k n) -> p k n", k=2)
        hid = v_raw[:, 0:2 * FB].rearrange("p (k n) -> p k n", k=2)
        y_t = m_pl[:, :, :].rearrange("p j n -> p (j n)")[:, 0:FB]
        wt_hl = ct_hi[0:2 * EX, :, :].rearrange("p c n -> p (c n)")[:, 0:B * T]
        sel = ct_lo[0:2 * EX, :, :].rearrange("p c n -> p (c n)")[:, 0:EX * 128].rearrange("p (e m) -> p e m", e=EX)
        gt = p_flat[:, 0:8 * PAIRS * EX].rearrange("p (k q e) -> p k q e", k=8, e=EX)
        w_hl = p_flat[:, 8 * PAIRS * EX:10 * PAIRS * EX].rearrange("p (q e) -> p q e", q=PAIRS)
        g1 = sb("g1", [PT, 7, PAIRS])
        gi = sb("gi", [PT, PAIRS, 8], U32)
        wgt_b = (p_s[:, :, :].rearrange("p g n -> p (g n)")[:, 10 * PAIRS * EX:10 * PAIRS * EX + FB],
                 qk_prod[:, :, :].rearrange("p h c -> p (h c)")[:, 0:FB])
        w_h = sb("w_h", [PT, PAIRS, EX], F32R)
        fin = sb("fin", [PT, PPB, C])
        out_s = sb("out_s", [PT, PPB, C])
        st3 = sb("st3", [PT, PPB, 6])
        mv3 = sb("mv3", [PT, PPB, 2])
        rstd3 = sb("rstd3", [PT, 2, PPB])
        wq_f = p_s[0:XD, :, :].rearrange("p g n -> p (g n)")[:, 0:XH * C].rearrange("p (h c) -> p h c", h=XH)
        wk_f = p_s[0:XD, :, :].rearrange("p g n -> p (g n)")[:, XH * C:XH * (C + CX)].rearrange("p (h c) -> p h c", h=XH)
        wv_f = u_flat[0:XD, 0:XH * CX].rearrange("p (h c) -> p h c", h=XH)
        wo_f = v_raw[0:XD, 0:XH * C].rearrange("p (h c) -> p h c", h=XH)

        ps_a = [ps(f"ps_a{n}", [128, 512]) for n in range(2)]
        ps_b = [ps(f"ps_b{n}", [128, 2, 512]) for n in range(2)]
        ps_u = ps("ps_u", [128, 512])
        side_ps = ps("side", [128, 512])

        up_banks = (ps_b[0][:, 0, :], ps_b[0][:, 1, :], ps_b[1][:, 1, :])
        fin_bank = side_ps[0:PT, :]

        cst_ld, sw_ld, xw_ld, swp_ld, bias_ld, gw_ld, w_ld, xt_ld, xn_ld, v_ld, out_st = (sem(n) for n in (
            "cst_ld", "sw_ld", "xw_ld", "swp_ld", "bias_ld", "gw_ld", "w_ld", "xt_ld", "xn_ld", "v_ld", "out_st"))
        ct_ld = [sem(f"ct_ld{c}") for c in range(3)]
        zeroed, pads_set, masks_set, prod_full, qk_set, vo_set, w_hi_set, w_split = (sem(n) for n in (
            "zeroed", "pads_set", "masks_set", "prod_full", "qk_set", "vo_set", "w_hi_set", "w_split"))
        side_full, side_free = sem("side_full"), sem("side_free")
        rows_set = sem("rows_set")
        a_full, a_max, b_full, pv_done = (sem(n) for n in ("a_full", "a_max", "b_full", "pv_done"))
        exp_hi, exp_raw, plo_set = (sem(n) for n in ("exp_hi", "exp_raw", "plo_set"))
        negm_set, xq_hi_set, u_set = (sem(n) for n in ("negm_set", "xq_hi_set", "u_set"))
        cthi_set, ctlo_set, vhi_set, vlo_set = (sem(n) for n in ("cthi_set", "ctlo_set", "vhi_set", "vlo_set"))
        q_hi_set, k_hi_set, rl_set, st1_set, mv1_set, ve1_set, rstd1_set, x1_set, xr_set, xb_set = (sem(n) for n in (
            "q_hi_set", "k_hi_set", "rl_set", "st1_set", "mv1_set", "ve1_set", "rstd1_set", "x1_set", "xr_set", "xb_set"))
        ry_set, y_summed, st2_set, mv2_set, ve2_set, rstd2_set, x2_set, x2_kept, x2t_hi_set = (
            sem(n) for n in ("ry_set", "y_summed", "st2_set", "mv2_set", "ve2_set", "rstd2_set", "x2_set",
                             "x2_kept", "x2t_hi_set"))
        gw_hi_set, gw_lo_set, sel_set, logits_full, gate_step, gate_exp, wt_full, wt_set = (sem(n) for n in (
            "gw_hi_set", "gw_lo_set", "sel_set", "logits_full", "gate_step", "gate_exp", "wt_full", "wt_set"))
        g_full, up_full, wb_full, wb_set, silu_set, weighted, hid_set, hid_hi_set, hid_lo_set, down_done = (
            sem(n) for n in ("g_full", "up_full", "wb_full", "wb_set", "silu_set", "weighted", "hid_set", "hid_hi_set",
                             "hid_lo_set", "down_done"))
        y_set, fin_full, fin_set, st3_set, mv3_set, ve3_set, rstd3_set, out_set = (sem(n) for n in (
            "y_set", "fin_full", "fin_set", "st3_set", "mv3_set", "ve3_set", "rstd3_set", "out_set"))

        def bits(ap):
            return ap.bitcast(F32)

        def over(ap, shape):
            return ap.broadcast_to(shape)

        def iterate(eng, body, first, loop_from, loop_to, last):
            for i in range(first, loop_from):
                body(i)
            with eng.Fori(loop_from, loop_to) as i:
                body(i)
            for i in range(loop_to, last):
                body(i)

        def alternates(i, step):
            return isinstance(i, int) and (i == -2 or (i == -1 and step < 22))

        def side_bank(i, step, group):
            return ps_u if alternates(i, step) and group % 2 else side_ps

        def at_last(i):
            return isinstance(i, int) and i == PAIRS - 1

        def at_end(i):
            return isinstance(i, int) and i == PAIRS

        def first_block(c):
            return isinstance(c, int) and c == 0

        def gate_stage(stages, at):
            return stages.get(at, "")

        def logits_of(part):
            first, last = GATE_PAIRS[part]
            bank = side_ps if part else ps_a[0]
            return bank[0:PT, 0:(last - first) * EX].rearrange("p (q e) -> p q e", e=EX)

        def exists(n, count=B, first=0):
            return not isinstance(n, int) or first <= n < count

        def wait(eng, s, n):
            if not isinstance(n, int) or n > 0:
                eng.wait_ge(s, n)

        def take_wait(eng):
            if eng is nc.vector:
                nc.vector.memset(spare[:, 0:1], 0.0)
            else:
                taken[0] = taken[0] % 31 + 1
                nc.gpsimd.tensor_tensor(spare[:, taken[0]:taken[0] + 1], eps[:, 0:1], eps[:, 0:1], ALU.add)

        block = ctx.enter_context(nc.Block())

        @block.sync
        def _(sp):
            sp.dma_start(swq[:, :, :, :], s_wq_t.rearrange("c (g j d) -> c g j d", g=SG, j=SJ)).then_inc(sw_ld, 16)
            sp.dma_start(swkv[:, :, :, :], s_wkv_t.rearrange("c (n g d) -> c n g d", n=2, g=SG)).then_inc(sw_ld, 16)
            sp.dma_start(xt[:, :], x_t[:, 0:PT]).then_inc(xt_ld, 16)
            sp.dma_start(cst[:, :], consts).then_inc(cst_ld, 16)
            for dst, src in ((wq_f, x_wq_t), (wk_f, x_wk_t), (wv_f, x_wv_t), (wo_f, x_wo)):
                sp.dma_start(dst, src.rearrange("(h d) c -> d h c", h=XH)).then_inc(xw_ld, 16)
            sp.dma_start(xn[:, :], x_n[0:PT, :]).then_inc(xn_ld, 16)
            sp.dma_start(swp[:, :], s_wp_t).then_inc(swp_ld, 16)
            sp.dma_start(bias2[:, :, :], s_bias.rearrange("p (n c) -> p n c", n=2)).then_inc(bias_ld, 16)
            for c in range(3):
                sp.dma_start(ct_raw[0:CX, c, :], ctx_t[0:CX, c * CHUNK:(c + 1) * CHUNK]).then_inc(ct_ld[c], 16)
            sp.dma_start(gw[:, :], gate_w).then_inc(gw_ld, 16)
            sp.dma_start(w_raw[:, :], w_all[:, 0:W_PIECE]).then_inc(w_ld, 16)
            sp.wait_ge(prod_full, 2)
            sp.dma_start(v_raw_t, ctx_n[0:KT, :].rearrange("p (t c) -> p t c", t=NT)).then_inc(v_ld, 16)

            def body(i):
                if isinstance(i, int) and i == -2:
                    sp.wait_ge(side_free, side_count(-2, S0K_STEP) + 1)
                    sp.dma_start(xt[:, :], x_t[:, PT:2 * PT]).then_inc(xt_ld, 16)
                    return
                for s in range(2):
                    n = 2 * i + s
                    if exists(n + 2, first=1):
                        wait(sp, ctlo_set, 3 * (n + 1) + 3)
                        sp.dma_start(ct_raw[0:CX, 2, :], ctx_t[bass.ds((n + 2) * CX, CX), 2 * CHUNK:3 * CHUNK])\
                          .then_inc(ct_ld[2], 16)
                    if s == 0 and exists(i + 2, PAIRS):
                        wait(sp, xr_set, i + 2)
                        sp.dma_start(xn[:, :], x_n[bass.ds((i + 2) * PT, PT), :]).then_inc(xn_ld, 16)
                    for c in range(2):
                        if exists(n + 3, first=1):
                            wait(sp, ctlo_set, 3 * (n + 2) + c + 1)
                            sp.dma_start(ct_raw[0:CX, c, :],
                                         ctx_t[bass.ds((n + 3) * CX, CX), c * CHUNK:(c + 1) * CHUNK])\
                              .then_inc(ct_ld[c], 16)
                        if c == 0 and exists(n + 2, first=1):
                            wait(sp, vlo_set, n + 2)
                            sp.dma_start(v_raw_t, ctx_n[bass.ds((n + 2) * KT, KT), :]
                                         .rearrange("p (t c) -> p t c", t=NT)).then_inc(v_ld, 16)
                    if s == 1 and exists(i + 1, PAIRS, 1):
                        sp.wait_ge(w_split, i + 1)
                        sp.dma_start(w_raw[:, :], w_all[:, bass.ds((i + 1) * W_PIECE, W_PIECE)]).then_inc(w_ld, 16)
                    if s == 1 and exists(i + 3, PAIRS):
                        sp.wait_ge(side_free, side_count(i, S0K_STEP) + 1)
                        sp.dma_start(xt[:, :], x_t[:, bass.ds((i + 3) * PT, PT)]).then_inc(xt_ld, 16)

            iterate(sp, body, -2, LOOP_FROM, PAIRS - 3, PAIRS)

            def store(c):
                sp.wait_ge(out_set, PPB * (c + 1))
                sp.dma_start(out[bass.ds(c * FB, FB), :].rearrange("(q p) n -> p q n", p=PT),
                             out_s[:, :, :]).then_inc(out_st, 16)

            iterate(sp, store, 0, 0, NB, NB)
            sp.wait_ge(out_st, 16 * NB)

        @block.tensor
        def _(pe):
            mm = nc.tensor.matmul

            def weight_product(dst, stationary, moving, width):
                for h in range(XH):
                    ins = mm(dst[:, h // 4, (h % 4) * width:(h % 4 + 1) * width], stationary[:, h, :], moving[:, h, :],
                             start=True, stop=True)
                ins.then_inc(prod_full, 1)

            def maxima(n, s, k):
                chunk, rows = k // 4, k % 4
                if k == 0:
                    pe.wait_ge(xq_hi_set, n + 1)
                if rows == 0:
                    pe.wait_ge(cthi_set, 3 * n + chunk + 1)
                wait(pe, a_max, 12 * n + k - 1)
                mm(ps_a[k % 2][0:PT, 0:CHUNK], xq_hi[0:CX, s, rows * PT:(rows + 1) * PT],
                   ct_hi[0:CX, s, chunk * CHUNK:(chunk + 1) * CHUNK], start=True, stop=True).then_inc(a_full, 1)

            def scores(i, s, t):
                n, u = 2 * i + s, t // 2
                if t == 0:
                    pe.wait_ge(side_free, (side_count(i, 10) if s else side_count_before(i, 22)) + 1)
                if t == 0 and isinstance(i, int) and i == 0 and s == 0:
                    pe.wait_ge(qk_set, 1)
                    pe.wait_ge(vo_set, 1)
                if t % 4 == 0:
                    pe.wait_ge(ctlo_set, 3 * n + t // 4 + 1)
                if t % 2 == 0:
                    wait(pe, plo_set, 6 * n + u - 1)
                dst = ps_b[u % 2][0:KT, t % 2, 0:XR]
                keys = slice(t * KT, (t + 1) * KT)
                mm(dst, ct_hi[:, s, keys], xq_hi[:, s, :], start=True, stop=False)
                mm(dst, ct_hi[0:CX, s, keys], xq_lo[:, s, :], start=False, stop=False)
                ins = mm(dst, ct_lo[:, s, keys], xq_hi[0:CX, s, :], start=False, stop=True)
                if t % 2:
                    ins.then_inc(b_full, 1)

            def sums(n, s, u, k):
                t = 2 * u + k
                if k == 0:
                    pe.wait_ge(plo_set, 6 * n + u + 1)
                if t == 0:
                    pe.wait_ge(vlo_set, n + 1)
                    wait(pe, u_set, n)
                mm(ps_u[0:CX + 1, 0:XR], v_hi[:, s, t, :], p_hi[u % 3][0:KT, k, :],
                   start=(t == 0), stop=False, skip_group_check=True)
                mm(ps_u[0:CX + 1, 0:XR], v_hi[:, s, t, :], p_lo[u % 3][0:KT, k, :],
                   start=False, stop=False, skip_group_check=True)
                ins = mm(ps_u[0:CX, 0:XR], v_lo[:, s, t, :], p_hi[u % 3][0:KT, k, :],
                         start=False, stop=(t == NT - 1), skip_group_check=True)
                if k:
                    ins.then_inc(pv_done, 1)

            def values(heads):
                for h in heads:
                    g, j = h // SJ, h % SJ
                    ins = mm(side_ps[0:PT, h * (SD + 1):(h + 1) * (SD + 1)], p_s[0:PT, g, j * PT:(j + 1) * PT],
                             v_s[:, g, :], start=True, stop=True)
                return ins

            def side_work(i, step, name):
                group = {"S1": S1_GROUP, "S3": S3_GROUP}.get(name, {}).get(step, 0)
                two_banks = alternates(i, step) and group > 0
                wait(pe, side_free, side_count(i, step) - (1 if two_banks else 0))
                side = side_bank(i, step, group)
                if name == "S0q":
                    pe.wait_ge(xt_ld, 16 * (i + 3))
                    if isinstance(i, int) and i == -2:
                        pe.wait_ge(pads_set, 6)
                    for j in range(SJ):
                        ins = mm(side[:, j * PT:(j + 1) * PT], wq_pad[:, j, :, :].rearrange("c g r -> c (g r)"),
                                 xt[:, :], start=True, stop=True)
                elif name == "S0k":
                    mm(side[:, 0:PT], wk_pad[:, :, :].rearrange("c g r -> c (g r)"), xt[:, :], start=True, stop=True)
                    ins = mm(side[0:PT, 128:128 + SG * SD], xt[:, :],
                             swkv[:, 1, :, :].rearrange("c g d -> c (g d)"), start=True, stop=True)
                elif name == "S1":
                    g = S1_GROUP[step]
                    if isinstance(i, int) and i == -2 and g == 0:
                        pe.wait_ge(masks_set, 3)
                    mm(side[0:PT, 0:SJ * PT], ident_b[0:PT, :], mask_b[:, 0, :, :].rearrange("p j n -> p (j n)"),
                       start=True, stop=False, skip_group_check=True)
                    for j in range(SJ):
                        ins = mm(side[0:PT, j * PT:(j + 1) * PT], q_s[32 * g:32 * g + 32, j * PT:(j + 1) * PT],
                                 k_s[32 * g:32 * g + 32, :], start=False, stop=(j == SJ - 1), skip_group_check=True)
                elif name == "S2":
                    for j in range(SJ):
                        ins = nc.tensor.transpose(side[:, j * PT:(j + 1) * PT], m_pl[0:PT, j, :], ident[0:PT, 0:PT])
                elif name == "S3":
                    g = S3_GROUP[step]
                    mm(side[0:PT, 0:SJ * PT], ident_b[0:PT, :], mask_b[:, 1, :, :].rearrange("p j n -> p (j n)"),
                       start=True, stop=False, skip_group_check=True)
                    ins = mm(side[0:PT, 0:SJ * PT], k_s[32 * g:32 * g + 32, :], q_m[32 * g:32 * g + 32, :],
                             start=False, stop=True, skip_group_check=True)
                elif name == "S4":
                    ins = values(range(2 * SJ, SH))
                elif name == "S5":
                    ins = nc.tensor.transpose(side[:, 0:PT], o_s[:, :], ident[0:PT, 0:PT])
                elif name == "S6":
                    if isinstance(i, int) and i == -1:
                        pe.wait_ge(swp_ld, 16)
                    ins = mm(side[0:PT, 0:C], o_t[:, :], swp[:, :], start=True, stop=True)
                elif name == "S7":
                    pe.wait_ge(x1_set, i + 2)
                    ins = nc.tensor.transpose(side[:, 0:PT], x1[:, :], ident[0:PT, 0:PT])
                elif name == "S8":
                    s = 0 if step else 1
                    if isinstance(i, int) and i == -1:
                        pe.wait_ge(qk_set, 1)
                    for h in range(XH):
                        ins = mm(side[0:CX, h * T:(h + 1) * T], qk_prod[:, h, :], x1t[:, s * T:(s + 1) * T],
                                 start=True, stop=True)
                elif name == "mrow":
                    pe.wait_ge(negm_set, 2 * i + step // 12 + 2)
                    for r in range(4):
                        ins = mm(side[CX:CX + 1, r * PT:(r + 1) * PT], negm[:, r:r + 1], ident[0:PT, 0:PT],
                                 start=True, stop=True)
                elif name[0] == "Y":
                    if step == 5:
                        pe.wait_ge(u_set, 2 * i)
                    for k, h in enumerate(Y_HEADS[step]):
                        ins = mm(side[0:PT, k * (C + 1):(k + 1) * (C + 1)], u_s[0:CX + 1, h, :], vo_prod[:, h, :],
                                 start=True, stop=True)
                elif name == "X2T":
                    pe.wait_ge(x2_set, i)
                    ins = nc.tensor.transpose(side[:, 0:PT], x2[:, :], ident[0:PT, 0:PT])
                ins.then_inc(side_full, 1)

            def gate_logits(part):
                if part == 0:
                    pe.wait_ge(gw_lo_set, 1)
                    pe.wait_ge(a_max, 12 * B)
                else:
                    pe.wait_ge(side_free, SIDE_END)
                dst = logits_of(part)
                for q in range(*GATE_PAIRS[part]):
                    cols, to = slice(q * PT, (q + 1) * PT), dst[:, q - GATE_PAIRS[part][0], :]
                    mm(to, x2t[0][:, cols], gw_hl[0][:, :], start=True, stop=False, skip_group_check=True)
                    mm(to, x2t[0][:, cols], gw_hl[1][:, :], start=False, stop=False, skip_group_check=True)
                    ins = mm(to, x2t[1][:, cols], gw_hl[0][:, :], start=False, stop=True, skip_group_check=True)
                ins.then_inc(logits_full, 1)

            def weights_t(c, bank):
                for q in range(PPB):
                    ins = nc.tensor.transpose(bank[0:2 * EX, q * PT:(q + 1) * PT], w_hl[:, c * PPB + q, :],
                                              ident[0:PT, 0:PT])
                ins.then_inc(wt_full, 1)

            def pair_step(i, step):
                here = parts(i)
                s, t = step // 12, step % 12
                if isinstance(i, int) and (i, step) == (-2, 16):
                    pe.wait_ge(xw_ld, 64)
                    weight_product(ps_b[0], wq_f, wk_f, CX)
                if isinstance(i, int) and (i, step) == (-2, 18):
                    weight_product(ps_b[1][0:CX, :, :], wv_f, wo_f, C)
                if "main" in here:
                    scores(i, s, t)
                for at, name, part in SIDE:
                    if at == step and part in here:
                        side_work(i, step, name)
                if step == 3 and "second" in here:
                    wait(pe, side_free, side_count(i, 4))
                    values(range(2 * SJ))
                if ("second" if s else "main") in here:
                    for k in MAXIMA.get(step, ()):
                        maxima(2 * i + s + 1, 1 - s, k)
                if step < 4 and "post" in here:
                    sums(2 * i - 1, 1, 4 + t // 2, t % 2)
                elif step >= 4 and "main" in here:
                    v = step - 4
                    sums(2 * i + v // 12, v // 12, v % 12 // 2, v % 2)
                if at_last(i) and gate_stage(GATE_STAGES, step) == "logits":
                    gate_logits(0)
                if at_end(i) and step == 3:
                    pe.wait_ge(sel_set, 1)
                    pe.wait_ge(gate_step, ALL_LINKS)
                    for c in range(NB - 1):
                        wait(pe, wt_set, c - 1)
                        weights_t(c, ps_b[1][:, c % 2, :])

            def body(i):
                for step in range(24):
                    pair_step(i, step)

            iterate(pe, body, -2, LOOP_FROM, LOOP_TO, PAIRS)
            for step in range(5):
                pair_step(PAIRS, step)

            pe.wait_ge(w_split, PAIRS)
            pe.wait_ge(gate_step, 2)
            pe.wait_ge(u_set, B)
            w_bank = ps_b[1][:, 0, :]

            def expert(c, q):
                e, half = EXPERTS[q // 2], q % 2
                main, late = exists(c, NB), (exists(c, NB) if q >= 3 else exists(c, NB + 1, 1))
                n = UNITS * c + q
                if first_block(c) and q in LAST_STEPS:
                    pair_step(PAIRS, LAST_STEPS[q])
                if first_block(c) and gate_stage(GATE_UNITS, q) == "logits":
                    gate_logits(1)
                if isinstance(c, int) and (c, q) == (1, 9):
                    pe.wait_ge(gate_step, 2 * ALL_LINKS)
                    pe.wait_ge(fin_set, 1)
                    weights_t(NB - 1, side_ps)
                if main:
                    if first_block(c) and q == 2:
                        pe.wait_ge(wt_set, NB - 1)
                    if isinstance(c, int) and (c, q) == (1, 12):
                        pe.wait_ge(wt_set, NB)
                    cols = slice((2 * e + half) * 128, (2 * e + half + 1) * 128)
                    moving = [part[:, bass.ds(c * FB, FB)] for part in x2t]
                    if e < EX and half == 0:
                        wait(pe, wb_set, EX * c + e)
                    for dst, w, used, full in ((ps_a[q % 2], wsp[0], silu_set, g_full),
                                               (up_banks[q % 3], wsp[1], hid_set, up_full)):
                        wait(pe, used, n - (1 if used is silu_set else 2))
                        dst = dst[:, 0:FB]
                        mm(dst, w[0][:, cols], moving[0], start=True, stop=False)
                        mm(dst, w[0][:, cols], moving[1], start=False, stop=False)
                        mm(dst, w[1][:, cols], moving[0], start=False, stop=True).then_inc(full, 1)
                        if w is wsp[0] and e < EX and half == 0:
                            mm(w_bank[:, 0:FB], sel[:, e, :], wt_hl[:, bass.ds(c * FB, FB)],
                               start=True, stop=True).then_inc(wb_full, 1)
                if late:
                    r = (q - 3) % UNITS
                    e, half = EXPERTS[r // 2], r % 2
                    cols = slice((2 * e + half) * 128, (2 * e + half + 1) * 128)
                    pe.wait_ge(hid_lo_set, n - 2)
                    if r == 0:
                        wait(pe, y_set, c)
                    h_hi, h_lo = p_hi[r % 3][:, 0, :], p_lo[r % 3][:, 0, :]
                    dst = ps_u[:, 0:FB]
                    mm(dst, wsp[2][0][:, cols], h_hi, start=(r == 0), stop=False, skip_group_check=True)
                    mm(dst, wsp[2][0][:, cols], h_lo, start=False, stop=False, skip_group_check=True)
                    mm(dst, wsp[2][1][:, cols], h_hi, start=False, stop=(r == UNITS - 1), skip_group_check=True)\
                        .then_inc(down_done, 1)
                if q == 4 and exists(c, NB + 1, 1):
                    pe.wait_ge(y_set, c)
                    wait(pe, fin_set, c - 1)
                    for k in range(PPB):
                        ins = nc.tensor.transpose(fin_bank[:, k * C:(k + 1) * C], y_t[:, k * PT:(k + 1) * PT], ident)
                    ins.then_inc(fin_full, 1)

            def experts(c):
                for q in range(UNITS if exists(c, NB) else 12):
                    expert(c, q)

            iterate(pe, experts, 0, 2, NB, NB + 1)

        @block.scalar
        def _(act):
            act_f = nc.scalar.activation

            def copy(dst, src):
                return act_f(dst, src, ACT.Copy)

            def split_weights(i):
                cols = bass.ds(i * W_PIECE, W_PIECE)
                act.wait_ge(w_ld, 16 * (i + 1))
                copy(w_hi[:, cols], w_raw[:, :]).then_inc(w_hi_set, 1)

            def exp_first(n, u):
                act.wait_ge(b_full, 6 * n + u + 1)
                wait(act, pv_done, 6 * n + u - 2)
                act_f(p_hi[u % 3][0:KT, :, :], ps_b[u % 2][0:KT, :, 0:XR], ACT.Exp, scale=X_SCALE).then_inc(exp_hi, 1)

            def exp_second(n, u):
                act.wait_ge(exp_hi, 6 * n + u + 1)
                b = ps_b[u % 2][0:KT, :, 0:XR]
                act_f(b, b, ACT.Exp, scale=X_SCALE).then_inc(exp_raw, 1)

            def side_work(i, step, name):
                if name in ("S4", "S6", "S1", "S2") or name[0] == "Y":
                    return
                act.wait_ge(side_full, side_count(i, step) + 1)
                side = side_bank(i, step, S3_GROUP[step] if name == "S3" else 0)
                if name == "S0q":
                    copy(q_hi[:, :], side[:, 0:SJ * PT]).then_inc(q_hi_set, 1)
                elif name == "S0k":
                    act_f(k_hi[:, :], side[:, 0:PT], ACT.Identity, bias=k_ones).then_inc(k_hi_set, 1)
                elif name == "S3":
                    act_f(p_s[0:PT, S3_GROUP[step], :], side[0:PT, 0:SJ * PT], ACT.Exp, scale=S_SCALE)\
                        .then_inc(side_free, 1)
                elif name == "S5":
                    copy(o_t[:, :], side[:, 0:PT]).then_inc(side_free, 1)
                elif name == "S7":
                    copy(x1t[:, :], side[:, 0:PT]).then_inc(side_free, 1)
                elif name == "S8":
                    copy(xq_hi[0:CX, 1 - step // 12, :], side[0:CX, 0:XR]).then_inc(xq_hi_set, 1)
                elif name == "mrow":
                    copy(xq_hi[CX:CX + 1, 1 - step // 12, :], side[CX:CX + 1, 0:XR]).then_inc(side_free, 1)
                elif name == "X2T":
                    copy(x2t[0][:, bass.ds((i - 1) * PT, PT)], side[:, 0:PT]).then_inc(x2t_hi_set, 1)

            def split_ct(n, s, c):
                act.wait_ge(ct_ld[c], 16 * (n + 1))
                wait(act, b_full, 6 * (n - 2) + 2 * c + 2)
                copy(ct_hi[0:CX, s, c * CHUNK:(c + 1) * CHUNK], ct_raw[0:CX, c, :]).then_inc(cthi_set, 1)

            def split_v(n, s, part):
                tiles = slice(part * 4, part * 4 + 4)
                if part == 0:
                    act.wait_ge(v_ld, 16 * (n + 1))
                    wait(act, pv_done, 6 * (n - 1))
                copy(v_hi[:, s, tiles, 0:CX], v_raw_t[:, tiles, :]).then_inc(vhi_set, 1)

            def save_sums(n, s):
                act.wait_ge(pv_done, 6 * (n + 1))
                copy(u_s[0:CX + 1, :, s * T:(s + 1) * T],
                     ps_u[0:CX + 1, 0:XR].rearrange("p (h t) -> p h t", h=XH)).then_inc(u_set, 1)

            def gate_exponentials(part):
                pairs = slice(*GATE_PAIRS[part])
                act.wait_ge(gate_step, part * ALL_LINKS + 2)
                act_f(gt[:, 1, pairs, :], gt[:, 0, pairs, :], ACT.Exp).then_inc(gate_exp, 1)

            def copy_weights(c, bank):
                act.wait_ge(wt_full, c + 1)
                copy(wt_hl[:, c * FB:(c + 1) * FB], bank[0:2 * EX, 0:FB]).then_inc(wt_set, 1)

            def pair_step(i, step):
                here = parts(i)
                s, t = step // 12, step % 12
                if isinstance(i, int) and (i, step) == (-2, 17):
                    act.wait_ge(prod_full, 1)
                    copy(qk_prod[:, :, :].rearrange("p (a h) c -> p a (h c)", a=2), ps_b[0][:, :, 0:4 * CX])\
                        .then_inc(qk_set, 1)
                if isinstance(i, int) and (i, step) == (-1, 13):
                    act.wait_ge(gw_ld, 16)
                    copy(gw_hl[0][:, :], gw[:, :]).then_inc(gw_hi_set, 1)
                if t % 2 and "main" in here:
                    exp_first(2 * i + s, t // 2)
                if t % 2 == 0:
                    if step == 0 and "post" in here:
                        exp_second(2 * i - 1, 5)
                    elif step and "main" in here:
                        exp_second(2 * i + (step - 1) // 12, (t // 2 - 1) % 6)
                if step == 4 and "post" in here:
                    save_sums(2 * i - 1, 1)
                if step == 16 and "main" in here:
                    save_sums(2 * i, 0)
                for at, name, part in SIDE:
                    if at == step and part in here:
                        side_work(i, step, name)
                if step == W_STEP and "main" in here:
                    split_weights(i)
                n = 2 * i + s
                if isinstance(i, int) and i == -2:
                    return
                if t == 0 and exists(n + 1):
                    split_ct(n + 1, 1 - s, 2)
                if t in (4, 8) and exists(n + 2):
                    split_ct(n + 2, s, t // 4 - 1)
                if t in (5, 7, 10) and exists(n + 1):
                    split_v(n + 1, 1 - s, (5, 7, 10).index(t))
                if at_last(i) and gate_stage(GATE_STAGES, step) == "exponentials":
                    gate_exponentials(0)
                if at_end(i) and step == 4:
                    for c in range(NB - 1):
                        copy_weights(c, ps_b[1][:, c % 2, :])

            def body(i):
                for step in range(24):
                    pair_step(i, step)

            iterate(act, body, -2, LOOP_FROM, LOOP_TO, PAIRS)
            for step in range(5):
                pair_step(PAIRS, step)

            def expert(c, q):
                e, half = EXPERTS[q // 2], q % 2
                n = UNITS * c + q
                if q == 3 and exists(c, NB + 1, 1):
                    act.wait_ge(down_done, UNITS * c)
                    wait(act, fin_full, c - 1)
                    copy(y_t, ps_u[:, 0:FB]).then_inc(y_set, 1)
                if first_block(c) and q in LAST_STEPS:
                    pair_step(PAIRS, LAST_STEPS[q])
                if first_block(c) and gate_stage(GATE_UNITS, q) == "exponentials":
                    gate_exponentials(1)
                if isinstance(c, int) and (c, q) == (1, 9):
                    copy_weights(NB - 1, side_ps)
                if exists(c, NB):
                    act.wait_ge(g_full, n + 1)
                    wait(act, hid_set, n - 1)
                    act_f(silu_s[:, q % 2, :], ps_a[q % 2][:, 0:FB], ACT.Silu).then_inc(silu_set, 1)
                    if e < EX and half == 0:
                        act.wait_ge(wb_full, EX * c + e + 1)
                        wait(act, weighted, 2 * (EX * c + e - 1))
                        copy(wgt_b[e % 2], ps_b[1][:, 0, 0:FB]).then_inc(wb_set, 1)
                if exists(c, NB) if q else exists(c, NB + 1, 1):
                    r = (q - 1) % UNITS
                    act.wait_ge(hid_set, n)
                    wait(act, down_done, n - 3)
                    copy(p_hi[r % 3][:, 0, :], hid[:, r % 2, :]).then_inc(hid_hi_set, 1)

            def experts(c):
                for q in range(UNITS if exists(c, NB) else 12):
                    expert(c, q)

            iterate(act, experts, 0, 2, NB, NB + 1)

        @block.vector
        def _(dve):
            tt, ts, stt, cp = nc.vector.tensor_tensor, nc.vector.tensor_scalar, nc.vector.scalar_tensor_tensor, \
                nc.vector.tensor_copy
            dve.wait_ge(sw_ld, 32)
            dve.wait_ge(zeroed, 8)
            for r in range(3):
                cp(wq_pad[:, :, :, r * SD:(r + 1) * SD],
                   swq[:, :, :, :].rearrange("c g j d -> c j g d")).then_inc(pads_set, 1)
                cp(wk_pad[:, :, r * SD:(r + 1) * SD], swkv[:, 0, :, :]).then_inc(pads_set, 1)
            dve.wait_ge(cst_ld, 16)
            cp(ident_b[:, :], ident[:, 0:PT]).then_inc(masks_set, 1)
            for m in range(2):
                cp(mask_b[:, m, :, :], over(cst[0:PT, None, 131 + m * PT:131 + (m + 1) * PT], [PT, SJ, PT]))\
                    .then_inc(masks_set, 1)

            def lo_parts(i, step):
                if step == 0 and "post" in parts(i):
                    probs_lo(2 * i - 1, 5)
                elif step and "main" in parts(i):
                    probs_lo(2 * i + (step - 1) // 12, (step % 12 // 2 - 1) % 6)

            def maxima(n, k):
                dve.wait_ge(a_full, 12 * n + k + 1)
                nc.vector.tensor_reduce(mx[:, k % 4, k // 4:k // 4 + 1], ps_a[k % 2][0:PT, 0:CHUNK], AX.X,
                                        ALU.max).then_inc(a_max, 1)
                if k == 11:
                    dve.wait_ge(a_max, 12 * (n + 1))
                    nc.vector.tensor_reduce(negm[:, :], mx[:, :, :], AX.X, ALU.max, negate=True).then_inc(negm_set, 1)

            def probs_lo(n, u):
                dve.wait_ge(exp_raw, 6 * n + u + 1)
                tt(p_lo[u % 3][0:KT, :, :], ps_b[u % 2][0:KT, :, 0:XR], bits(p_hi[u % 3][0:KT, :, :]),
                   ALU.subtract).then_inc(plo_set, 1)

            def statistics(src, st, mv, n, st_set, mv_set):
                nc.vector.bn_stats(st[:, :], src[:, :]).then_inc(st_set, 1)
                dve.wait_ge(st_set, n)
                take_wait(nc.vector)
                nc.vector.bn_aggr(mv[:, :], st[:, :]).then_inc(mv_set, 1)

            def side_work(i, step, name):
                use = side_count(i, step)
                side = side_bank(i, step, S1_GROUP[step] if name == "S1" else 0)
                if name in ("S3", "S5", "S7", "mrow"):
                    return
                if name not in ("S0q", "S0k", "S8", "X2T"):
                    dve.wait_ge(side_full, use + 1)
                if name == "S0q":
                    dve.wait_ge(q_hi_set, i + 3)
                    stt(q_s[:, :], bits(q_hi[:, :]), q_part, side[:, 0:SJ * PT], ALU.mult, ALU.add)\
                        .then_inc(side_free, 1)
                elif name == "S0k":
                    dve.wait_ge(k_hi_set, i + 3)
                    stt(k_s[:, :], bits(k_hi[:, :]), k_part, side[:, 0:PT], ALU.mult, ALU.add)
                    cp(v_s[:, :, 0:SD], side[0:PT, 128:128 + SG * SD].rearrange("p (g d) -> p g d", g=SG))\
                        .then_inc(side_free, 1)
                elif name == "S1":
                    at = 32 * S1_GROUP[step] + MAX_ROW
                    nc.vector.tensor_reduce(m_pl[0:PT, :, at:at + 1],
                                            side[0:PT, 0:SJ * PT].rearrange("p (j n) -> p j n", j=SJ), AX.X, ALU.max,
                                            negate=True).then_inc(side_free, 1)
                elif name == "S2":
                    tt(q_m[:, :], side[:, 0:SJ * PT], bits(q_s[:, :]), ALU.add).then_inc(side_free, 1)
                elif name == "S4":
                    o = side[0:PT, 0:SH * (SD + 1)].rearrange("p (h d) -> p h d", h=SH)
                    nc.vector.reciprocal(rl_s[:, :], side[0:PT, SD:SH * (SD + 1):SD + 1]).then_inc(rl_set, 1)
                    dve.wait_ge(rl_set, i + 2)
                    tt(o_s[:, :].rearrange("p (h d) -> p h d", h=SH), o[:, :, 0:SD],
                       over(rl_s[:, :, None], [PT, SH, SD]), ALU.mult).then_inc(side_free, 1)
                elif name == "S6":
                    dve.wait_ge(xr_set, i + 2)
                    tt(r1[:, :], side[0:PT, 0:C], xr[:, :], ALU.add).then_inc(side_free, 1)
                elif name == "S8":
                    buffer = 1 - step // 12
                    dve.wait_ge(xq_hi_set, 2 * i + step // 12 + 2)
                    tt(xq_lo[:, buffer, :], side[0:CX, 0:XR], bits(xq_hi[0:CX, buffer, :]), ALU.subtract)\
                        .then_inc(side_free, 1)
                elif name[0] == "Y":
                    heads = Y_HEADS[step]
                    first, count = heads[0], len(heads)
                    if step == 5:
                        wait(dve, y_summed, 4 * (i - 1))
                    nc.vector.reciprocal(ry[:, 0:count], side[0:PT, C:count * (C + 1):C + 1]).then_inc(ry_set, 1)
                    dve.wait_ge(ry_set, 3 * (i - 1) + list(Y_HEADS).index(step) + 1)
                    tt(y_h[:, first:first + count, :],
                       side[0:PT, 0:count * (C + 1)].rearrange("p (h c) -> p h c", h=count)[:, :, 0:C],
                       over(ry[:, 0:count, None], [PT, count, C]), ALU.mult).then_inc(side_free, 1)
                elif name == "X2T":
                    dve.wait_ge(x2t_hi_set, i)
                    cols = bass.ds((i - 1) * PT, PT)
                    tt(x2t[1][:, cols], side[:, 0:PT], bits(x2t[0][:, cols]), ALU.subtract).then_inc(side_free, 1)

            links = [0]

            def link(ins):
                links[0] += 1
                ins.then_inc(gate_step, 1)
                dve.wait_ge(gate_step, links[0])

            def gate(part, stage):
                first, last = GATE_PAIRS[part]
                g, t, full = g1[:, :, first:last], gt[:, :, first:last, :], [PT, last - first, EX]
                if stage == "differences":
                    dve.wait_ge(logits_full, part + 1)
                    link(nc.vector.tensor_reduce(g[:, 0, :], logits_of(part), AX.X, ALU.max, negate=True))
                    link(tt(t[:, 0, :, :], logits_of(part), over(g[:, 0, :, None], full), ALU.add))
                elif stage == "probabilities":
                    dve.wait_ge(gate_exp, part + 1)
                    link(nc.vector.tensor_reduce(g[:, 1, :], t[:, 1, :, :], AX.X, ALU.add))
                    link(nc.vector.reciprocal(g[:, 2, :], g[:, 1, :]))
                    link(tt(t[:, 2, :, :], t[:, 1, :, :], over(g[:, 2, :, None], full), ALU.mult))
                elif stage == "largest":
                    for q in range(first, last):
                        ins = nc.vector.max(gt[:, 3, q, :], gt[:, 2, q, :])
                    link(ins)
                    for q in range(first, last):
                        ins = nc.vector.max_index(gi[:, q, :], gt[:, 3, q, :], gt[:, 2, q, :])
                    link(ins)
                elif stage == "shares":
                    link(cp(t[:, 4, :, :], gi[:, first:last, :]))
                    link(tt(g[:, 3, :], t[:, 3, :, 0], t[:, 3, :, 1], ALU.add))
                    link(ts(g[:, 4, :], g[:, 3, :], 1e-20, None, ALU.add))
                    link(nc.vector.reciprocal(g[:, 5, :], g[:, 4, :]))
                elif stage in ("first", "second"):
                    k = ("first", "second").index(stage)
                    link(tt(g[:, 6, :], t[:, 3, :, k], g[:, 5, :], ALU.mult))
                    link(tt(t[:, 5 + k, :, :], over(iota8[:, None, :], full), over(t[:, 4, :, k:k + 1], full),
                            ALU.is_equal))
                    link(tt(t[:, 5 + k, :, :], t[:, 5 + k, :, :], over(g[:, 6, :, None], full), ALU.mult))
                elif stage == "split":
                    link(tt(t[:, 7, :, :], t[:, 5, :, :], t[:, 6, :, :], ALU.add))
                    link(cp(w_h[:, first:last, :], t[:, 7, :, :]))
                    link(cp(w_hl[:, first:last, 0:EX], bits(w_h[:, first:last, :])))
                    link(tt(w_hl[:, first:last, EX:2 * EX], t[:, 7, :, :], bits(w_h[:, first:last, :]), ALU.subtract))

            def pair_step(i, step):
                here = parts(i)
                s, t = step // 12, step % 12
                if isinstance(i, int) and (i, step) == (-2, 19):
                    dve.wait_ge(prod_full, 2)
                    cp(vo_prod[0:CX, :, 0:C], ps_b[1][0:CX, :, :].rearrange("p a (h c) -> p (a h) c", h=4))\
                        .then_inc(vo_set, 1)
                    nc.vector.memset(vo_prod[CX:CX + 1, :, 0:C], 0.0).then_inc(rows_set, 1)
                    nc.vector.memset(vo_prod[CX:CX + 1, :, C:C + 1], 1.0).then_inc(rows_set, 1)
                if isinstance(i, int) and i == -1 and step in (3, 5):
                    buffer = (step - 3) // 2
                    nc.vector.memset(bits(ct_hi[CX:CX + 1, buffer, :]), 1.0).then_inc(rows_set, 1)
                if isinstance(i, int) and (i, step) == (-1, 14):
                    dve.wait_ge(gw_hi_set, 1)
                    tt(gw_hl[1][:, :], gw[:, :], bits(gw_hl[0][:, :]), ALU.subtract).then_inc(gw_lo_set, 1)
                if t % 2 == 0 and step not in SIDE_FIRST:
                    lo_parts(i, step)
                for at, name, part in SIDE:
                    if at == step and part in here:
                        side_work(i, step, name)
                if step == 9 and "second" in here:
                    dve.wait_ge(side_free, side_count(i, 8) + 1)
                    statistics(r1, st1, mv1, i + 2, st1_set, mv1_set)
                if step == 10 and "second" in here:
                    dve.wait_ge(rstd1_set, i + 2)
                    wait(dve, xb_set, i + 1)
                    ts(x1[:, :], r1[:, :], mv1[:, 0:1], rstd1[:, 1:2], ALU.subtract, ALU.mult).then_inc(x1_set, 1)
                if step in SIDE_FIRST:
                    lo_parts(i, step)
                if step == 15 and "post" in here:
                    dve.wait_ge(y_summed, 4 * i)
                    statistics(acc, st2, mv2, i, st2_set, mv2_set)
                if step == 17 and "post" in here:
                    dve.wait_ge(rstd2_set, i)
                    wait(dve, x2_kept, i - 1)
                    ts(x2[:, :], acc[:, :], mv2[:, 0:1], rstd2[:, 1:2], ALU.subtract, ALU.mult).then_inc(x2_set, 1)
                if ("second" if s else "main") in here:
                    for k in MAXIMA.get(step, ()):
                        maxima(2 * i + s + 1, k)
                if at_last(i):
                    gate(0, gate_stage(GATE_STAGES, step))
                if at_end(i) and step == 1:
                    tt(sel, over(ident[0:2 * EX, 0:EX, None], [2 * EX, EX, 128]),
                       over(ident[0:2 * EX, EX:2 * EX, None], [2 * EX, EX, 128]), ALU.add).then_inc(sel_set, 1)

            def body(i):
                for step in range(24):
                    pair_step(i, step)

            iterate(dve, body, -2, LOOP_FROM, LOOP_TO, PAIRS)
            for step in range(5):
                pair_step(PAIRS, step)

            def expert(c, q):
                e = EXPERTS[q // 2]
                n = UNITS * c + q
                if first_block(c) and q in LAST_STEPS:
                    pair_step(PAIRS, LAST_STEPS[q])
                if isinstance(c, int) and c < 2:
                    gate(1, gate_stage(GATE_UNITS, UNITS * c + q))
                if exists(c, NB):
                    if e < EX:
                        dve.wait_ge(weighted, 2 * EX * c + q - 1)
                    else:
                        dve.wait_ge(silu_set, n + 1)
                    dve.wait_ge(up_full, n + 1)
                    wait(dve, hid_lo_set, n - 1)
                    tt(hid[:, q % 2, :], silu_s[:, q % 2, :], up_banks[q % 3][:, 0:FB], ALU.mult).then_inc(hid_set, 1)
                if exists(c, NB) if q else exists(c, NB + 1, 1):
                    r = (q - 1) % UNITS
                    dve.wait_ge(hid_hi_set, n)
                    tt(p_lo[r % 3][:, 0, :], hid[:, r % 2, :], bits(p_hi[r % 3][:, 0, :]), ALU.subtract)\
                        .then_inc(hid_lo_set, 1)
                if q == 5 and exists(c, NB + 1, 1):
                    dve.wait_ge(fin_full, c)
                    tt(fin[:, :, :].rearrange("p q n -> p (q n)"), fin_bank,
                       x_rows[:, bass.ds((c - 1) * PPB * C, PPB * C)], ALU.add).then_inc(fin_set, 1)
                if q == 6 and exists(c, NB + 1, 1):
                    dve.wait_ge(fin_set, c)
                    for k in range(PPB):
                        ins = nc.vector.bn_stats(st3[:, k, :], fin[:, k, :])
                    ins.then_inc(st3_set, 1)
                if q == 7 and exists(c, NB + 1, 1):
                    dve.wait_ge(st3_set, c)
                    take_wait(nc.vector)
                    for k in range(PPB):
                        ins = nc.vector.bn_aggr(mv3[:, k, :], st3[:, k, :])
                    ins.then_inc(mv3_set, 1)
                if q in (10, 11) and exists(c, NB + 1, 1):
                    dve.wait_ge(rstd3_set, c)
                    wait(dve, out_st, 16 * (c - 1))
                    for k in range(PPB // 2 * (q - 10), PPB // 2 * (q - 9)):
                        ts(out_s[:, k, :], fin[:, k, :], mv3[:, k, 0:1], rstd3[:, 1, k:k + 1],
                           ALU.subtract, ALU.mult).then_inc(out_set, 1)

            def experts(c):
                for q in range(UNITS if exists(c, NB) else 12):
                    expert(c, q)

            iterate(dve, experts, 0, 2, NB, NB + 1)

        @block.gpsimd
        def _(pool):
            ptt, pcp, fill = nc.gpsimd.tensor_tensor, nc.gpsimd.tensor_copy, nc.gpsimd.memset
            for ap, value in ((wq_pad[:, :, :, :], 0.0), (wk_pad[:, :, :], 0.0), (m_pl[:, :, :], 0.0),
                              (v_s[:, :, :], 1.0), (eps[:, :], EPS), (nhalf[:, :], -0.5),
                              (vo_prod[0:CX, :, C:C + 1], 0.0), (bits(v_hi[:, :, :, CX:CX + 1]), 1.0)):
                fill(ap, value).then_inc(zeroed, 1)
            pool.wait_ge(zeroed, 8)

            def split_ct(n, s, c):
                cols = slice(c * CHUNK, (c + 1) * CHUNK)
                pool.wait_ge(cthi_set, 3 * n + c + 1)
                ptt(ct_lo[:, s, cols], ct_raw[0:CX, c, :], bits(ct_hi[0:CX, s, cols]), ALU.subtract)\
                    .then_inc(ctlo_set, 1)

            def split_v(n, s, part):
                tiles = slice(part * 4, part * 4 + 4)
                pool.wait_ge(vhi_set, 3 * n + part + 1)
                ins = ptt(v_lo[:, s, tiles, :], v_raw_t[:, tiles, :], bits(v_hi[:, s, tiles, 0:CX]), ALU.subtract)
                if part == 2:
                    ins.then_inc(vlo_set, 1)

            def rstd(out2, var, n, ve_set, done):
                width = out2[0].shape[-1]
                ptt(out2[0], var, eps[0:PT, 0:width], ALU.add).then_inc(ve_set, 1)
                pool.wait_ge(ve_set, n)
                ptt(out2[1], out2[0], nhalf[0:PT, 0:width], ALU.pow).then_inc(done, 1)

            def pair_step(i, step):
                here = parts(i)
                s, t = step // 12, step % 12
                n = 2 * i + s
                if t == 0 and exists(n + 1):
                    split_ct(n + 1, 1 - s, 2)
                if t in (4, 8) and exists(n + 2):
                    split_ct(n + 2, s, t // 4 - 1)
                if t in (5, 7, 10) and exists(n + 1):
                    split_v(n + 1, 1 - s, (5, 7, 10).index(t))
                if step == W_STEP + 1 and "main" in here:
                    cols = bass.ds(i * W_PIECE, W_PIECE)
                    pool.wait_ge(w_hi_set, i + 1)
                    ptt(w_lo[:, cols], w_raw[:, :], bits(w_hi[:, cols]), ALU.subtract).then_inc(w_split, 1)
                if step == 3 and "second" in here:
                    if isinstance(i, int) and i == -1:
                        pool.wait_ge(bias_ld, 16)
                    pool.wait_ge(xn_ld, 16 * (i + 2))
                    wait(pool, mv1_set, i + 1)
                    ptt(xr[:, :], xn[:, :], bias2[:, 0, :], ALU.add).then_inc(xr_set, 1)
                if step == 9 and "second" in here:
                    pool.wait_ge(mv1_set, i + 2)
                    rstd((rstd1[:, 0:1], rstd1[:, 1:2]), mv1[:, 1:2], i + 2, ve1_set, rstd1_set)
                if step == 11 and "second" in here:
                    pool.wait_ge(x1_set, i + 2)
                    ptt(x_rows[:, bass.ds((i + 1) * C, C)], x1[:, :], bias2[:, 1, :], ALU.add).then_inc(xb_set, 1)
                if step == 12 and "post" in here:
                    pool.wait_ge(side_free, side_count(i, 9) + 1)
                    ptt(y_h[:, 0:4, :], y_h[:, 0:4, :], y_h[:, 4:8, :], ALU.add).then_inc(y_summed, 1)
                if step == 13 and "post" in here:
                    for k, half in enumerate((2, 1)):
                        pool.wait_ge(y_summed, 4 * (i - 1) + k + 1)
                        ptt(y_h[:, 0:half, :], y_h[:, 0:half, :], y_h[:, half:2 * half, :], ALU.add)\
                            .then_inc(y_summed, 1)
                    pool.wait_ge(y_summed, 4 * (i - 1) + 3)
                    wait(pool, x2_set, i - 1)
                    ptt(acc[:, :], y_h[:, 0, :], x_rows[:, bass.ds((i - 1) * C, C)], ALU.add).then_inc(y_summed, 1)
                if step == 16 and "post" in here:
                    pool.wait_ge(mv2_set, i)
                    rstd((rstd2[:, 0:1], rstd2[:, 1:2]), mv2[:, 1:2], i, ve2_set, rstd2_set)
                if step == 18 and "post" in here:
                    pool.wait_ge(x2_set, i)
                    take_wait(nc.gpsimd)
                    pcp(x_rows[:, bass.ds((i - 1) * C, C)], x2[:, :]).then_inc(x2_kept, 1)

            def body(i):
                for step in range(0 if isinstance(i, int) and i == -2 else 24):
                    pair_step(i, step)

            iterate(pool, body, -2, LOOP_FROM, LOOP_TO, PAIRS)

            def expert(c, q):
                e, half = EXPERTS[q // 2], q % 2
                if first_block(c) and q in LAST_STEPS:
                    pair_step(PAIRS, LAST_STEPS[q])
                if exists(c, NB) and e < EX:
                    pool.wait_ge(silu_set, UNITS * c + q + 1)
                    pool.wait_ge(wb_set, EX * c + e + 1)
                    ptt(silu_s[:, q % 2, :], silu_s[:, q % 2, :], wgt_b[e % 2], ALU.mult).then_inc(weighted, 1)
                if q == 9 and exists(c, NB + 1, 1):
                    pool.wait_ge(mv3_set, c)
                    rstd((rstd3[:, 0, :], rstd3[:, 1, :]), mv3[:, :, 1], c, ve3_set, rstd3_set)

            def experts(c):
                for q in range(UNITS if exists(c, NB) else 12):
                    expert(c, q)

            iterate(pool, experts, 0, 2, NB, NB + 1)


def constants():
    cst = np.zeros((128, CONST_COLS), np.float32)
    cst[:, 0:128] = np.eye(128)
    row = np.arange(128) % 32
    cst[:, 128] = np.where((row >= SD) & (row < 2 * SD), -1.0, 0.0)
    cst[:, 129] = np.where((row >= 2 * SD) & (row < 3 * SD), -1.0, 0.0)
    cst[:, 129] += np.where(row == MAX_ROW, 1.0, 0.0)
    cst[:, 130] = np.where(row == MAX_ROW, 1.0, 0.0)
    q, k = np.arange(PT)[:, None], np.arange(PT)[None, :]
    mask = np.where((q // T == k // T) & (k <= q), 0.0, MASKED)
    cst[0:PT, 131:131 + PT] = mask
    cst[0:PT, 131 + PT:131 + 2 * PT] = mask.T
    cst[:, 131 + 2 * PT:] = np.arange(EX)
    return cst


def kernel(**inputs):
    import concourse.bacc as bacc
    from concourse.bass_utils import run_bass_kernel_spmd

    a = {n: np.asarray(v) for n, v in inputs.items()}
    x = a["x"].reshape(B * T, C)
    context = a["ctx_768"].reshape(B, KT, NT, CX)
    shared = {n: a["L0_ffn_ws_" + n] for n in ("gate", "up", "down")}
    wide = {n: np.concatenate([a["L0_ffn_w_" + n], shared[n][None]]).transpose(1, 0, 2).reshape(C, -1)
            for n in ("gate", "up")}
    down = np.concatenate([a["L0_ffn_w_down"], shared["down"][None]]).reshape(EX + 1, 2, 128, C)
    s_bias = np.concatenate([a["L0_attn_bp"], a["L0_xattn_bo"]])
    arrays = {
        "x_t": x.T, "x_n": x,
        "ctx_n": context.reshape(B * KT, NT * CX),
        "ctx_t": context.transpose(0, 3, 2, 1).reshape(B * CX, KV),
        "s_wq_t": a["L0_attn_Wq"].reshape(SH * SD, C).T,
        "s_wkv_t": np.concatenate([a["L0_attn_Wk"].reshape(SG * SD, C), a["L0_attn_Wv"].reshape(SG * SD, C)]).T,
        "s_wp_t": a["L0_attn_Wp"].T,
        "s_bias": np.broadcast_to(s_bias, (PT, 2 * C)),
        "x_wq_t": a["L0_xattn_Wq"].T, "x_wk_t": a["L0_xattn_Wk"].T, "x_wv_t": a["L0_xattn_Wv"].T,
        "x_wo": a["L0_xattn_Wo"],
        "gate_w": a["L0_ffn_gate_w"],
        "w_all": np.concatenate([wide["gate"], wide["up"], down.transpose(2, 0, 1, 3).reshape(128, -1)], axis=1),
        "consts": constants(),
    }
    nc = bacc.Bacc("TRN2", target_bir_lowering=False, num_devices=1)
    feeds, args = {}, []
    for name, value in arrays.items():
        value = np.ascontiguousarray(value)
        feeds["in_" + name] = value
        args.append(nc.dram_tensor("in_" + name, value.shape, mybir.dt.from_np(value.dtype), kind="ExternalInput").ap())
    out = nc.dram_tensor("out", (B * T, C), F32, kind="ExternalOutput").ap()
    bass_decoder_layer(nc, *args, out)
    result = run_bass_kernel_spmd(nc, [feeds], core_ids=[0])
    return result.results[0]["out"].reshape(B, T, C)
```
